# Optimizing a Trainium2 kernel written in Bass

```python
import numpy as np
import jax
import jax.numpy as jnp

def _softmax(x, axis=-1):
    return jax.nn.softmax(x, axis=axis)

def _gelu(x):
    return jax.nn.gelu(x, approximate=True)

def _silu(x):
    return jax.nn.silu(x)

def _sigmoid(x):
    return jax.nn.sigmoid(x)

def _layernorm(x, axis=-1, eps=1e-05):
    m = jnp.mean(x, axis=axis, keepdims=True)
    v = jnp.var(x, axis=axis, keepdims=True)
    return (x - m) / jnp.sqrt(v + eps)

def _scatter_add(tgt, idx, src, axis=0):
    return tgt.at[idx].add(src)

def _segment_sum(src, seg, n):
    return jax.ops.segment_sum(src, seg, n)
kernel_name = 'mk_flamingo_gated_d2_seqx_r8_3366ba'

def setup_inputs(seed: int=0):
    np.random.seed(seed)
    _w = jnp.asarray

    def _rec_inputs():
        import jax
        import jax.numpy as jnp
        _rk = jax.random.key(seed)
        x = -0.0002928 + 1 * jax.random.normal(jax.random.fold_in(_rk, 1), (16, 256, 128), jnp.float32)
        _lenS = 256 - jax.random.randint(jax.random.fold_in(_rk, 7), (16,), 0, max(1, 256 // 4) + 1, jnp.int32)
        _lenS2 = 64 - jax.random.randint(jax.random.fold_in(_rk, 8), (16,), 0, max(1, 64 // 4) + 1, jnp.int32)
        _ctx_1024P = jax.random.normal(jax.random.fold_in(_rk, 11), (16, 16, 128), jnp.float32)
        _ctx_1024c = jax.random.dirichlet(jax.random.fold_in(_rk, 511), 0.3 * jnp.ones((16,), jnp.float32), (16, 64))
        _ctx_1024t = jnp.einsum('bsk,bkd->bsd', _ctx_1024c, _ctx_1024P)
        _ctx_1024t = _ctx_1024t * jax.lax.rsqrt(jnp.mean(jnp.square(_ctx_1024t)) + 1e-12) * 0.953939
        ctx_1024 = -1.39393e-06 + 0.999914 * (_ctx_1024t + 0.3 * jax.random.normal(jax.random.fold_in(_rk, 611), (16, 64, 128), jnp.float32))
        _validS = jnp.arange(256)[None, :] < _lenS[:, None]
        _validS2 = jnp.arange(64)[None, :] < _lenS2[:, None]
        _causal = jnp.tril(jnp.ones((256, 256), dtype=bool))
        mask_BxS2_bf0 = jnp.logical_not(jnp.ones((16, 64), dtype=bool))
        mask_BxS2_bk0 = jnp.logical_not(jnp.broadcast_to(_validS2[:, :], (16, 64)))
        _g = jax.random.normal(jax.random.fold_in(_rk, 9001), (2, 2), jnp.float32)
        _g = jnp.sign(_g) * jnp.maximum(jnp.abs(_g), 1.0) + (_g == 0) * 1.0
        g_xattn = _g[0]
        g_ffn = _g[1]
        return (x, ctx_1024, mask_BxS2_bf0, mask_BxS2_bk0, g_xattn, g_ffn)
    x, ctx_1024, mask_BxS2_bf0, mask_BxS2_bk0, g_xattn, g_ffn = _rec_inputs()

    def _L0_xattn_setup():
        import jax, jax.numpy as jnp
        import numpy as np
        B, N, D = (2, 256, 128)
        H = 16
        HC = D // H
        ROPE_BASE = 10000.0

        def _rope(x):
            c = x.shape[-1]
            n = x.shape[-2]
            inv_freq = 1.0 / ROPE_BASE ** (jnp.arange(0, c, 2, dtype=jnp.float32) / c)
            t = jnp.arange(n, dtype=jnp.float32)[:, None] * inv_freq[None, :]
            cos = jnp.repeat(jnp.cos(t), 2, axis=-1).astype(x.dtype)
            sin = jnp.repeat(jnp.sin(t), 2, axis=-1).astype(x.dtype)
            x1 = x[..., ::2]
            x2 = x[..., 1::2]
            x_rot = jnp.stack([-x2, x1], axis=-1).reshape(x.shape)
            return x * cos + x_rot * sin
        key = jax.random.key(seed)
        ks = jax.random.split(key, 10)
        s_in = 1.0 / np.sqrt(D)
        return {'x_q': jax.random.normal(ks[0], (B, N, D), jnp.float32), 'x_kv': jax.random.normal(ks[1], (B, N, D), jnp.float32), 'pad_mask': jnp.zeros((B, N), dtype=bool), 'Wq': jax.random.normal(ks[2], (D, D), jnp.float32) * s_in, 'bq': jnp.zeros((D,), jnp.float32), 'Wk': jax.random.normal(ks[3], (D, D), jnp.float32) * s_in, 'bk': jnp.zeros((D,), jnp.float32), 'Wv': jax.random.normal(ks[4], (D, D), jnp.float32) * s_in, 'bv': jnp.zeros((D,), jnp.float32), 'Wo': jax.random.normal(ks[5], (D, D), jnp.float32) * s_in, 'bo': jnp.zeros((D,), jnp.float32)}
    _L0_xattn_all = _L0_xattn_setup()
    _L0_xattn_in = {k: v for k, v in _L0_xattn_all.items() if k in ('Wq', 'bq', 'Wk', 'bk', 'Wv', 'bv', 'Wo', 'bo')}
    del _L0_xattn_all

    def _L0_ffn_setup():
        import jax, jax.numpy as jnp
        import numpy as np
        B, S, D, F, E, K = (4, 256, 128, 512, 4, 2)
        key = jax.random.key(seed)
        k = jax.random.split(key, 6)
        x = jax.random.normal(k[0], (B, S, D), jnp.float32)
        router_w = jax.random.normal(k[1], (D, E), jnp.float32) * D ** (-0.5)
        router_b = jnp.zeros((E,), jnp.float32)
        w1 = jax.random.normal(k[2], (E, D, F), jnp.float32) * 0.02
        w3 = jax.random.normal(k[3], (E, D, F), jnp.float32) * 0.02
        w2 = jax.random.normal(k[4], (E, F, D), jnp.float32) * 0.02
        return {'x': x, 'router_w': router_w, 'router_b': router_b, 'w1': w1, 'w3': w3, 'w2': w2}
    _L0_ffn_all = _L0_ffn_setup()
    _L0_ffn_in = {k: v for k, v in _L0_ffn_all.items() if k in ('router_w', 'router_b', 'w1', 'w3', 'w2')}
    del _L0_ffn_all

    def _L1_xattn_setup():
        import jax, jax.numpy as jnp
        import numpy as np
        DIM, DIM_HEAD, HEADS, SCALE = (128, 64, 8, 8.0)
        INNER = DIM_HEAD * HEADS
        LN_EPS = 1e-05
        L2_EPS = 1e-12

        def layer_norm(x, w, b):
            mu = jnp.mean(x, axis=-1, keepdims=True)
            var = jnp.mean(jnp.square(x - mu), axis=-1, keepdims=True)
            return (x - mu) * jax.lax.rsqrt(var + LN_EPS) * w + b

        def l2norm(t):
            n = jnp.sqrt(jnp.sum(jnp.square(t), axis=-1, keepdims=True))
            return t / jnp.maximum(n, L2_EPS)
        key = jax.random.key(seed)
        ks = jax.random.split(key, 8)
        b, n, m = (8, 1024, 64)
        x = jax.random.normal(ks[0], (b, n, DIM), dtype=jnp.float32)
        latents = jax.random.normal(ks[1], (b, m, DIM), dtype=jnp.float32)
        mask = jax.random.randint(ks[2], (b, n), 0, 2) > 0
        Wq = jax.random.normal(ks[3], (DIM, INNER), dtype=jnp.float32) * DIM ** (-0.5)
        Wkv = jax.random.normal(ks[4], (DIM, 2 * INNER), dtype=jnp.float32) * DIM ** (-0.5)
        Wo = jax.random.normal(ks[5], (INNER, DIM), dtype=jnp.float32) * INNER ** (-0.5)
        return {'x': x, 'latents': latents, 'mask': mask, 'ln_x_w': jnp.ones((DIM,)), 'ln_x_b': jnp.zeros((DIM,)), 'ln_l_w': jnp.ones((DIM,)), 'ln_l_b': jnp.zeros((DIM,)), 'Wq': Wq, 'Wkv': Wkv, 'q_scale': jnp.ones((DIM_HEAD,)), 'k_scale': jnp.ones((DIM_HEAD,)), 'Wo': Wo, 'ln_o_w': jnp.ones((DIM,)), 'ln_o_b': jnp.zeros((DIM,))}
    _L1_xattn_all = _L1_xattn_setup()
    _L1_xattn_in = {k: v for k, v in _L1_xattn_all.items() if k in ('ln_x_w', 'ln_x_b', 'ln_l_w', 'ln_l_b', 'Wq', 'Wkv', 'q_scale', 'k_scale', 'Wo', 'ln_o_w', 'ln_o_b')}
    del _L1_xattn_all

    def _L1_ffn_setup():
        import jax, jax.numpy as jnp
        import numpy as np
        E, K = (8, 4)
        B, S, D = (4, 128, 128)
        H = D * 2 * 4 // 3

        def _swiglu(u, w1, w2, w3):
            h = jnp.einsum('...d,hd->...h', u, w1)
            v = jnp.einsum('...d,hd->...h', u, w2)
            return jnp.einsum('...h,dh->...d', jax.nn.sigmoid(h) * h * v, w3)
        key = jax.random.key(seed)
        ks = jax.random.split(key, 9)
        std = 0.02
        return {'x': jax.random.normal(ks[0], (B, S, D), jnp.float32), 'Wg': jax.random.normal(ks[1], (E, D), jnp.float32) * std, 'routing_bias': jnp.zeros((E,), jnp.float32), 'W1': jax.random.normal(ks[2], (E, H, D), jnp.float32) * std, 'W2': jax.random.normal(ks[3], (E, H, D), jnp.float32) * std, 'W3': jax.random.normal(ks[4], (E, D, H), jnp.float32) * std, 'Ws1': jax.random.normal(ks[5], (H, D), jnp.float32) * std, 'Ws2': jax.random.normal(ks[6], (H, D), jnp.float32) * std, 'Ws3': jax.random.normal(ks[7], (D, H), jnp.float32) * std}
    _L1_ffn_all = _L1_ffn_setup()
    _L1_ffn_in = {k: v for k, v in _L1_ffn_all.items() if k in ('Wg', 'routing_bias', 'W1', 'W2', 'W3', 'Ws1', 'Ws2', 'Ws3')}
    del _L1_ffn_all
    return {'x': x, 'ctx_1024': ctx_1024, 'mask_BxS2_bf0': mask_BxS2_bf0, 'mask_BxS2_bk0': mask_BxS2_bk0, 'g_xattn': g_xattn, 'g_ffn': g_ffn, 'L0_xattn_Wq': _L0_xattn_in['Wq'], 'L0_xattn_bq': _L0_xattn_in['bq'], 'L0_xattn_Wk': _L0_xattn_in['Wk'], 'L0_xattn_bk': _L0_xattn_in['bk'], 'L0_xattn_Wv': _L0_xattn_in['Wv'], 'L0_xattn_bv': _L0_xattn_in['bv'], 'L0_xattn_Wo': _L0_xattn_in['Wo'], 'L0_xattn_bo': _L0_xattn_in['bo'], 'L0_ffn_router_w': _L0_ffn_in['router_w'], 'L0_ffn_router_b': _L0_ffn_in['router_b'], 'L0_ffn_w1': _L0_ffn_in['w1'], 'L0_ffn_w3': _L0_ffn_in['w3'], 'L0_ffn_w2': _L0_ffn_in['w2'], 'L1_xattn_ln_x_w': _L1_xattn_in['ln_x_w'], 'L1_xattn_ln_x_b': _L1_xattn_in['ln_x_b'], 'L1_xattn_ln_l_w': _L1_xattn_in['ln_l_w'], 'L1_xattn_ln_l_b': _L1_xattn_in['ln_l_b'], 'L1_xattn_Wq': _L1_xattn_in['Wq'], 'L1_xattn_Wkv': _L1_xattn_in['Wkv'], 'L1_xattn_q_scale': _L1_xattn_in['q_scale'], 'L1_xattn_k_scale': _L1_xattn_in['k_scale'], 'L1_xattn_Wo': _L1_xattn_in['Wo'], 'L1_xattn_ln_o_w': _L1_xattn_in['ln_o_w'], 'L1_xattn_ln_o_b': _L1_xattn_in['ln_o_b'], 'L1_ffn_Wg': _L1_ffn_in['Wg'], 'L1_ffn_routing_bias': _L1_ffn_in['routing_bias'], 'L1_ffn_W1': _L1_ffn_in['W1'], 'L1_ffn_W2': _L1_ffn_in['W2'], 'L1_ffn_W3': _L1_ffn_in['W3'], 'L1_ffn_Ws1': _L1_ffn_in['Ws1'], 'L1_ffn_Ws2': _L1_ffn_in['Ws2'], 'L1_ffn_Ws3': _L1_ffn_in['Ws3']}

def reference(x, ctx_1024, mask_BxS2_bf0, mask_BxS2_bk0, g_xattn, g_ffn, L0_xattn_Wq, L0_xattn_bq, L0_xattn_Wk, L0_xattn_bk, L0_xattn_Wv, L0_xattn_bv, L0_xattn_Wo, L0_xattn_bo, L0_ffn_router_w, L0_ffn_router_b, L0_ffn_w1, L0_ffn_w3, L0_ffn_w2, L1_xattn_ln_x_w, L1_xattn_ln_x_b, L1_xattn_ln_l_w, L1_xattn_ln_l_b, L1_xattn_Wq, L1_xattn_Wkv, L1_xattn_q_scale, L1_xattn_k_scale, L1_xattn_Wo, L1_xattn_ln_o_w, L1_xattn_ln_o_b, L1_ffn_Wg, L1_ffn_routing_bias, L1_ffn_W1, L1_ffn_W2, L1_ffn_W3, L1_ffn_Ws1, L1_ffn_Ws2, L1_ffn_Ws3):
    import jax
    import jax.numpy as jnp

    def _L0_xattn_ref(x_q, x_kv, pad_mask, Wq, bq, Wk, bk, Wv, bv, Wo, bo):
        import jax, jax.numpy as jnp
        import numpy as np
        B, N, D = (2, 256, 128)
        H = 16
        HC = D // H
        ROPE_BASE = 10000.0

        def _rope(x):
            c = x.shape[-1]
            n = x.shape[-2]
            inv_freq = 1.0 / ROPE_BASE ** (jnp.arange(0, c, 2, dtype=jnp.float32) / c)
            t = jnp.arange(n, dtype=jnp.float32)[:, None] * inv_freq[None, :]
            cos = jnp.repeat(jnp.cos(t), 2, axis=-1).astype(x.dtype)
            sin = jnp.repeat(jnp.sin(t), 2, axis=-1).astype(x.dtype)
            x1 = x[..., ::2]
            x2 = x[..., 1::2]
            x_rot = jnp.stack([-x2, x1], axis=-1).reshape(x.shape)
            return x * cos + x_rot * sin
        dp_scale = HC ** (-0.5)
        q = x_q @ Wq + bq
        k = x_kv @ Wk + bk
        v = x_kv @ Wv + bv

        def split_heads(x):
            b, n, _ = x.shape
            return x.reshape(b, n, H, -1).transpose(0, 2, 1, 3)
        q, k, v = (split_heads(q), split_heads(k), split_heads(v))
        q = q * dp_scale
        q = _rope(q)
        k = _rope(k)
        attn = jnp.einsum('bhic,bhjc->bhij', q, k)
        neg = -jnp.finfo(attn.dtype).max
        attn = jnp.where(pad_mask[:, None, None, :], neg, attn)
        i, j = (q.shape[2], k.shape[2])
        causal = jnp.triu(jnp.ones((i, j), dtype=bool), k=j - i + 1)
        attn = jnp.where(causal, neg, attn)
        attn = jax.nn.softmax(attn, axis=-1)
        o = jnp.einsum('bhij,bhjc->bhic', attn, v)
        b, h, n, c = o.shape
        o = o.transpose(0, 2, 1, 3).reshape(b, n, h * c)
        return o @ Wo + bo

    def _L0_ffn_ref(x, router_w, router_b, w1, w3, w2):
        import jax, jax.numpy as jnp
        import numpy as np
        B, S, D, F, E, K = (4, 256, 128, 512, 4, 2)
        b, s, d = x.shape
        T = b * s
        e = router_w.shape[1]
        xf = x.reshape(T, d)
        logits = xf @ router_w + router_b
        probs = jax.nn.softmax(logits, axis=-1)
        top_p, top_i = jax.lax.top_k(probs, K)
        top_p = top_p / jnp.sum(top_p, axis=-1, keepdims=True)
        gates = jnp.zeros((T, e), xf.dtype).at[jnp.arange(T)[:, None], top_i].add(top_p)
        h = jax.nn.silu(jnp.einsum('td,edf->etf', xf, w1)) * jnp.einsum('td,edf->etf', xf, w3)
        expert_out = jnp.einsum('etf,efd->etd', h, w2)
        out = jnp.einsum('te,etd->td', gates, expert_out)
        return out.reshape(b, s, d)

    def _L1_xattn_ref(x, latents, mask, ln_x_w, ln_x_b, ln_l_w, ln_l_b, Wq, Wkv, q_scale, k_scale, Wo, ln_o_w, ln_o_b):
        import jax, jax.numpy as jnp
        import numpy as np
        DIM, DIM_HEAD, HEADS, SCALE = (128, 64, 8, 8.0)
        INNER = DIM_HEAD * HEADS
        LN_EPS = 1e-05
        L2_EPS = 1e-12

        def layer_norm(x, w, b):
            mu = jnp.mean(x, axis=-1, keepdims=True)
            var = jnp.mean(jnp.square(x - mu), axis=-1, keepdims=True)
            return (x - mu) * jax.lax.rsqrt(var + LN_EPS) * w + b

        def l2norm(t):
            n = jnp.sqrt(jnp.sum(jnp.square(t), axis=-1, keepdims=True))
            return t / jnp.maximum(n, L2_EPS)
        b, n, _ = x.shape
        m = latents.shape[1]
        x = layer_norm(x, ln_x_w, ln_x_b)
        latents = layer_norm(latents, ln_l_w, ln_l_b)
        q = latents @ Wq
        kv_input = jnp.concatenate([x, latents], axis=1)
        kv = kv_input @ Wkv
        k, v = jnp.split(kv, 2, axis=-1)

        def to_heads(t):
            return t.reshape(t.shape[0], t.shape[1], HEADS, DIM_HEAD).transpose(0, 2, 1, 3)
        q, k, v = map(to_heads, (q, k, v))
        q = l2norm(q) * q_scale
        k = l2norm(k) * k_scale
        sim = jnp.einsum('bhid,bhjd->bhij', q, k) * SCALE
        full_mask = jnp.concatenate([mask, jnp.ones((b, m), dtype=bool)], axis=1)[:, None, None, :]
        max_neg = -jnp.finfo(sim.dtype).max
        sim = jnp.where(full_mask, sim, max_neg)
        attn = jax.nn.softmax(sim.astype(jnp.float32), axis=-1).astype(sim.dtype)
        out = jnp.einsum('bhij,bhjd->bhid', attn, v)
        out = out.transpose(0, 2, 1, 3).reshape(b, m, INNER)
        return layer_norm(out @ Wo, ln_o_w, ln_o_b)

    def _L1_ffn_ref(x, Wg, routing_bias, W1, W2, W3, Ws1, Ws2, Ws3):
        import jax, jax.numpy as jnp
        import numpy as np
        E, K = (8, 4)
        B, S, D = (4, 128, 128)
        H = D * 2 * 4 // 3

        def _swiglu(u, w1, w2, w3):
            h = jnp.einsum('...d,hd->...h', u, w1)
            v = jnp.einsum('...d,hd->...h', u, w2)
            return jnp.einsum('...h,dh->...d', jax.nn.sigmoid(h) * h * v, w3)
        gate = jnp.einsum('bsd,ed->bse', x, Wg) + routing_bias
        _, top_idx = jax.lax.top_k(gate, K)
        mask = jax.nn.one_hot(top_idx, E, dtype=gate.dtype).sum(-2)
        masked_gate = jnp.where(mask > 0, gate, -jnp.inf)
        probs = jax.nn.softmax(masked_gate, axis=-1)
        weights = probs * mask
        out = _swiglu(x, Ws1, Ws2, Ws3)
        h1 = jnp.einsum('bsd,ehd->ebsh', x, W1)
        h2 = jnp.einsum('bsd,ehd->ebsh', x, W2)
        eo = jnp.einsum('ebsh,edh->ebsd', jax.nn.sigmoid(h1) * h1 * h2, W3)
        out = out + jnp.einsum('ebsd,bse->bsd', eo, weights)
        return out
    x = x + jnp.tanh(g_xattn[0]) * _L0_xattn_ref(_layernorm(x, axis=-1), ctx_1024, mask_BxS2_bf0, L0_xattn_Wq, L0_xattn_bq, L0_xattn_Wk, L0_xattn_bk, L0_xattn_Wv, L0_xattn_bv, L0_xattn_Wo, L0_xattn_bo)
    x = x + jnp.tanh(g_ffn[0]) * _L0_ffn_ref(_layernorm(x, axis=-1), L0_ffn_router_w, L0_ffn_router_b, L0_ffn_w1, L0_ffn_w3, L0_ffn_w2)
    x = x + jnp.tanh(g_xattn[1]) * _L1_xattn_ref(ctx_1024, _layernorm(x, axis=-1), mask_BxS2_bk0, L1_xattn_ln_x_w, L1_xattn_ln_x_b, L1_xattn_ln_l_w, L1_xattn_ln_l_b, L1_xattn_Wq, L1_xattn_Wkv, L1_xattn_q_scale, L1_xattn_k_scale, L1_xattn_Wo, L1_xattn_ln_o_w, L1_xattn_ln_o_b)
    x = x + jnp.tanh(g_ffn[1]) * _L1_ffn_ref(_layernorm(x, axis=-1), L1_ffn_Wg, L1_ffn_routing_bias, L1_ffn_W1, L1_ffn_W2, L1_ffn_W3, L1_ffn_Ws1, L1_ffn_Ws2, L1_ffn_Ws3)
    return x

_drawn_inputs = setup_inputs


def setup_inputs(seed=0):
    import zlib

    import numpy as np

    out = dict(_drawn_inputs(seed))
    spreads = {'g_ffn': (-1.0, 0.6),
     'L0_xattn_bq': (0.0, 0.8),
     'L0_xattn_bk': (0.0, 0.8),
     'L0_xattn_bv': (0.0, 0.1),
     'L0_xattn_bo': (0.0, 0.1),
     'L0_ffn_router_b': (0.0, 0.8),
     'L1_xattn_ln_x_w': (1.0, 0.6),
     'L1_xattn_ln_x_b': (0.0, 0.71),
     'L1_xattn_ln_l_w': (1.0, 0.2),
     'L1_xattn_ln_l_b': (0.0, 0.1),
     'L1_xattn_q_scale': (1.0, 0.2),
     'L1_xattn_k_scale': (1.0, 0.2),
     'L1_xattn_ln_o_w': (1.0, 0.2),
     'L1_xattn_ln_o_b': (0.0, 0.347),
     'L1_ffn_routing_bias': (0.0, 0.8)}
    factors = {'L0_ffn_router_w': 8.0,
     'L0_ffn_w1': 8.0,
     'L0_ffn_w3': 8.0,
     'L0_ffn_w2': 8.0,
     'L1_ffn_Wg': 8.0,
     'L1_ffn_W1': 8.0,
     'L1_ffn_W2': 8.0,
     'L1_ffn_W3': 8.0,
     'L1_ffn_Ws1': 8.0,
     'L1_ffn_Ws2': 8.0,
     'L1_ffn_Ws3': 8.0}
    for name, (base, spread) in spreads.items():
        noise = np.random.default_rng([zlib.crc32(name.encode()), seed]).standard_normal(out[name].shape)
        drawn = base * np.exp(spread * noise) if base else spread * noise
        out[name] = jnp.asarray(drawn.astype(out[name].dtype))
    for name, factor in factors.items():
        out[name] = (out[name] * factor).astype(out[name].dtype)
    return out
```

```python
from contextlib import ExitStack

import concourse.bass as bass
import numpy as np
from concourse import mybir

F32 = mybir.dt.float32
F32R = mybir.dt.float32r
I32 = mybir.dt.int32
U8 = mybir.dt.uint8
ACT = mybir.ActivationFunctionType
ALU = mybir.AluOpType
AX = mybir.AxisListType

P = 128
NB, NT, NCTX = 16, 256, 64
TILES = NB * NT // P
BLK = 512
NBLK = NB * NT // BLK
H0, C0 = 16, 8
H1, C1 = 8, 64
F0, F1 = 512, 341
E0, K0, E1, K1 = 4, 2, 8, 4
QPOS = NT - NCTX
NEG = -float(np.finfo(np.float32).max)
LN_EPS = 1e-5
MAGIC = 0x5F3759DF

COLS = ["bq", "bq_swap", "bk", "bk_swap", "bv", "ln_l_w", "ln_l_b", "ln_x_w", "ln_x_b", "q_scale", "k_scale"]
ROWS = {"bo": P, "bv": P, "router_b": E0, "routing_bias": E1, "ln_o_w": P, "ln_o_b": P, "g": 4}
ROW_AT, _n = {}, 0
for _k, _w in ROWS.items():
    ROW_AT[_k] = (_n, _n + _w)
    _n += _w
NROWS = _n


class Chain:

    def __init__(self, sem):
        self.sem, self.base, self.k, self.round, self.per = sem, 0, 0, 0, 0

    def start(self, i, per):
        self.round, self.per, self.k = i, per, 0

    def value(self):
        return self.round * self.per + (self.base + self.k)

    def end_body(self):
        assert self.k == self.per, (self.k, self.per)

    def end(self, rounds):
        self.base += rounds * self.per
        self.round, self.per, self.k = 0, 0, 0

    def settle(self):
        self.base, self.k = self.base + self.k, 0


def constants():
    inv = (1.0 / np.float32(10000.0) ** (np.arange(0, C0, 2, dtype=np.float32) / C0)).astype(np.float32)
    t = np.arange(NT, dtype=np.float32)[:, None] * inv[None, :]
    cos = np.repeat(np.cos(t), 2, axis=1)
    sin = np.repeat(np.sin(t), 2, axis=1)
    sin[:, ::2] *= -1.0
    cos, sin = (np.tile(a, (1, H0)).T.astype(np.float32) for a in (cos, sin))
    scale = np.float32(C0 ** -0.5)
    rope = np.concatenate([cos[:, :NCTX], sin[:, :NCTX], cos[:, QPOS:] * scale, sin[:, QPOS:] * scale], 1)
    eye = np.eye(P, dtype=np.float32)
    p = np.arange(P)
    head_of = (p[:, None] // C0 % 4 == np.arange(4)[None, :]).astype(np.float32)
    vhalf = (p[:, None] // 64 == np.arange(16)[None, :] // C0).astype(np.float32)
    barred = (np.arange(NCTX)[None, :] > p[:, None] % 64).astype(np.float32)
    tri0, tri1 = (np.tile(np.tril(np.ones((n, n), np.float32), -1).reshape(1, n * n), (P, 1)) for n in (E0, E1))
    sel = np.zeros((P, (E0 + E1) * P), np.float32)
    for e in range(E0):
        sel[[e, E0 + e], e * P:(e + 1) * P] = 1.0
    for e in range(E1):
        sel[[e, E1 + e], (E0 + e) * P:(E0 + e + 1) * P] = 1.0
    return {"cst": np.ascontiguousarray(np.concatenate([rope, eye, head_of, vhalf, barred, tri0, tri1], 1)
                                        .astype(np.float32)), "sel": sel}


CST = {"cos_k": (0, 64), "sin_k": (64, 128), "cos_q": (128, 192), "sin_q": (192, 256), "eye": (256, 384),
       "head_of": (384, 388), "vhalf": (388, 404), "barred": (404, 468), "tri0": (468, 484), "tri1": (484, 548)}
NCST = CST["tri1"][1]


def lay_out(a):
    swap = np.arange(P) ^ 1
    f = lambda *parts: np.ascontiguousarray(np.concatenate(parts, 1))
    wq, wk = a["L0_xattn_Wq"], a["L0_xattn_Wk"]
    both = lambda v: np.tile(v, P // C1)
    colv = {"bq": a["L0_xattn_bq"], "bq_swap": a["L0_xattn_bq"][swap], "bk": a["L0_xattn_bk"],
            "bk_swap": a["L0_xattn_bk"][swap], "bv": a["L0_xattn_bv"], "ln_l_w": a["L1_xattn_ln_l_w"],
            "ln_l_b": a["L1_xattn_ln_l_b"], "ln_x_w": a["L1_xattn_ln_x_w"], "ln_x_b": a["L1_xattn_ln_x_b"],
            "q_scale": both(a["L1_xattn_q_scale"]), "k_scale": both(a["L1_xattn_k_scale"])}
    rowv = {"bo": a["L0_xattn_bo"], "bv": a["L0_xattn_bv"], "router_b": a["L0_ffn_router_b"],
            "routing_bias": a["L1_ffn_routing_bias"], "ln_o_w": a["L1_xattn_ln_o_w"], "ln_o_b": a["L1_xattn_ln_o_b"],
            "g": np.concatenate([a["g_xattn"], a["g_ffn"]])}
    pad, keep = a["mask_BxS2_bf0"], a["mask_BxS2_bk0"]
    cat9 = lambda shared, w: np.concatenate([shared[None], w])
    w1, w2 = (cat9(a[f"L1_ffn_Ws{n}"], a[f"L1_ffn_W{n}"]).transpose(2, 0, 1).reshape(P, -1) for n in (1, 2))
    w3 = np.zeros((E1 + 1, 3 * P, P), np.float32)
    w3[:, :F1] = cat9(a["L1_ffn_Ws3"], a["L1_ffn_W3"]).transpose(0, 2, 1)
    chunks = lambda w: w.reshape(w.shape[0], -1, P, P).transpose(2, 0, 1, 3).reshape(P, -1)
    return {
        "x": a["x"].reshape(NB * NT, P),
        "ctxT": np.ascontiguousarray(a["ctx_1024"].reshape(NB * NCTX, P).T),
        "ctx": np.ascontiguousarray(a["ctx_1024"].reshape(NB * NCTX, P)),
        "wA": f(wq, wq[:, swap], wk, wk[:, swap], a["L0_xattn_Wv"], a["L0_xattn_Wo"]).reshape(P, 6, P),
        **constants(),
        "rows": np.ascontiguousarray(np.broadcast_to(np.concatenate([rowv[k] for k in ROWS])[None], (P, NROWS))),
        "cols": np.ascontiguousarray(np.stack([colv[k] for k in COLS], 1)),
        "pad": np.ascontiguousarray(np.repeat(pad.reshape(NB // 2, 2, 1, NCTX), 64, 2).reshape(NB // 2, P, NCTX)
                                    .transpose(1, 0, 2)),
        "kmask": np.ascontiguousarray(np.broadcast_to(keep[None], (P, NB, NCTX))),
        "rw": f(a["L0_ffn_router_w"], a["L1_ffn_Wg"].T),
        "wo1": np.ascontiguousarray(a["L1_xattn_Wo"].reshape(4, P, P).transpose(1, 0, 2)),
        "w0": f(a["L0_ffn_w1"].transpose(1, 0, 2).reshape(P, -1), a["L0_ffn_w3"].transpose(1, 0, 2).reshape(P, -1),
                chunks(a["L0_ffn_w2"])),
        "wa": f(a["L1_xattn_Wq"], a["L1_xattn_Wkv"]),
        "w1": f(w1, w2, chunks(w3)),
    }


def ffn_plan(layer):
    if layer == 0:
        n, f, chunks = E0, F0, 4
    else:
        n, f, chunks = E1 + 1, F1, 3
    return [(e, c, min(P, f - c * P), e * f + c * P, n * f + e * f + c * P, 2 * n * f + (e * chunks + c) * P)
            for e in range(n) for c in range(chunks)]


class Layer:

    def __init__(self, layer, before=None, jobs=0):
        self.plan = ffn_plan(layer)
        self.units, self.experts, self.chunks = len(self.plan), self.plan[-1][0] + 1, self.plan[-1][1] + 1
        self.E, self.K, self.gated0 = (E0, K0, 0) if layer == 0 else (E1, K1, 1)
        self.rw0, self.sel0, self.g = (0, 0, 2) if layer == 0 else (2 * E0, E0, 3)
        self.bias, self.tri = ("router_b", "tri0") if layer == 0 else ("routing_bias", "tri1")
        self.jobs = jobs
        self.bufs, self.bufs32 = (4, 4) if layer == 0 else (3, 6)
        self.blocks = self.unit0 = self.expert0 = self.gates = self.adds = 0
        if before:
            self.blocks, self.unit0 = NBLK, NBLK * before.units
            self.expert0, self.gates = NBLK * before.experts, NBLK * before.E
            self.adds = NBLK * (before.experts - 1)


W0_COLS = 2 * E0 * F0 + E0 * 4 * P
W1_COLS = 2 * (E1 + 1) * F1 + (E1 + 1) * 3 * P
WA_COLS = 3 * H1 * C1
STAGE = 1024


STATS, GUESS, NEWTON, ROWS_IN, ACC_TURN, X_ADD, ROT = 0, 1, (2, 3, 4), 5, 5, 5, 6
X_TURN, X_HI, X_LO, LOGITS, LOGITS_IN, GATE_EXP, RANK, WEIGHTS, GATE_TURN, GATES_IN = \
    8, 8, 9, 11, 11, 12, 12, 13, 15, 15
LAG = 3
FREE_A, FREE_H, FREE_DOWN, FREE_YG, FREE_X, FREE_ACC = 1, 2, 4, 2, 1, 1


def split_jobs():
    jobs = []
    for src, dst, cols in (("w0", "w", W0_COLS), ("wa", "wa", WA_COLS), ("w1", "w", W1_COLS)):
        for at in range(0, cols, STAGE):
            jobs.append((src, at, dst, at, min(STAGE, cols - at)))
    return jobs


def build(nc, ins, out):
    ctx = ExitStack()
    JOBS = split_jobs()
    JOBS_B = sum(j[0] == "w0" for j in JOBS)
    JOBS_C = JOBS_B + sum(j[0] == "wa" for j in JOBS)
    L0 = Layer(0, jobs=JOBS_B)
    L1 = Layer(1, before=L0, jobs=len(JOBS))
    with ctx:
        def sb(name, shape, dt=F32, scope=ctx):
            return scope.enter_context(nc.sbuf_tensor(name, shape, dt))

        def sem(name):
            return ctx.enter_context(nc.semaphore(name))

        x = sb("x_res", [P, TILES, P])
        w_hi, w_lo = sb("w_hi", [P, W1_COLS], F32R), sb("w_lo", [P, W1_COLS], F32R)
        wa_hi, wa_lo = sb("wa_hi", [P, WA_COLS], F32R), sb("wa_lo", [P, WA_COLS], F32R)
        wo1 = sb("wo1", [P, 4, P])
        stage = sb("stage", [P, 2, STAGE])
        cst = sb("cst", [P, NCST])
        sel = sb("sel", [P, (E0 + E1) * P], F32R)
        rows = sb("rows", [P, NROWS])
        cols = sb("cols", [P, len(COLS)])
        rw = sb("rw", [P, E0 + E1])
        rw_r = sb("rw_r", [P, 2 * (E0 + E1)], F32R)
        pad = sb("pad", [P, NB // 2, NCTX], U8)
        kmask = sb("kmask", [P, NB, NCTX], U8)
        tg = sb("tg", [P, 4])
        stat = sb("stat", [P, 4, 6])
        mv = sb("mv", [P, 4, 2])
        rs = sb("rs", [P, 3, 48])
        hold = sb("hold", [P, 32])

        def C(name):
            a, b = CST[name]
            return cst[:, a:b]

        def col(name):
            k = COLS.index(name)
            return cols[:, k:k + 1]

        def row(name):
            a, b = ROW_AT[name]
            return rows[:, a:b]

        eye = C("eye")
        bank = [ctx.enter_context(nc.psum_tensor(f"bank{i}", [P, 512], F32)) for i in range(8)]

        xn = sb("xn", [P, 4, P])
        ctx_hi, ctx_lo = (sb(n, [P, NB * NCTX], F32R) for n in ("ctx_hi", "ctx_lo"))

        scope_a = ExitStack()
        ctxr = sb("ctxr", [P, NB // 2, P], scope=scope_a)
        ctx_stat, ctx_mv = sb("ctx_stat", [P, NB // 2, 6], scope=scope_a), sb("ctx_mv", [P, NB // 2, 2], scope=scope_a)
        q_stat, q_mv = sb("q_stat", [P, NB, 6], scope=scope_a), sb("q_mv", [P, NB, 2], scope=scope_a)
        q_rs = sb("q_rs", [P, 3, NB], scope=scope_a)
        ctx32 = sb("ctx32", [P, NB * NCTX], scope=scope_a)
        ctxT = sb("ctxT", [P, NB * NCTX], scope=scope_a)
        sel32 = sb("sel32", [P, (E0 + E1) * P], scope=scope_a)
        wA = sb("wA", [P, 6, P], scope=scope_a)
        krope = sb("krope", [P, NB * NCTX], scope=scope_a)
        ktmp = sb("ktmp", [P, 512], scope=scope_a)
        mneg = sb("mneg", [P, NB // 2, NCTX], scope=scope_a)
        mctx = sb("mctx", [P, NB], scope=scope_a)
        omT = sb("omT", [P, NB], scope=scope_a)
        xq = sb("xq", [P, 2, P], scope=scope_a)
        xqT = sb("xqT", [P, 2, NCTX], scope=scope_a)
        qr1, qr2, qT = (sb(n, [P, 2, NCTX], scope=scope_a) for n in ("qr1", "qr2", "qT"))
        ctxdup = sb("ctxdup", [P, 2, 2, NCTX], scope=scope_a)
        vtmp = sb("vtmp", [P, 2 * P], scope=scope_a)
        vbd = sb("vbd", [P, 2, 8, 16], scope=scope_a)
        kbd = sb("kbd", [P, 2, 4, NCTX], scope=scope_a)
        sm = sb("sm", [P, H0, NCTX], scope=scope_a)
        pr = sb("pr", [P, H0, NCTX], scope=scope_a)
        sred = sb("sred", [P, 3, H0], scope=scope_a)
        pT = sb("pT", [P, 8, P], scope=scope_a)
        on = sb("on", [P, P], scope=scope_a)
        oT = sb("oT", [P, 2, 2 * P], scope=scope_a)
        ytmp = sb("ytmp", [P, 4, P], scope=scope_a)
        scope_a.close()

        scope_f = ExitStack()
        xs_hi, xs_lo = (sb(n, [P, 2, BLK], F32R, scope=scope_f) for n in ("xs_hi", "xs_lo"))
        act_t = sb("act_t", [P, 2, BLK], scope=scope_f)
        h32 = sb("h32", [P, 6, BLK], scope=scope_f)
        h_hi, h_lo = (sb(n, [P, 4, BLK], F32R, scope=scope_f) for n in ("h_hi", "h_lo"))
        g_bc = sb("g_bc", [P, 2, BLK], scope=scope_f)
        yg = sb("yg", [P, 2, BLK], scope=scope_f)
        acc = sb("acc", [P, 2, BLK], scope=scope_f)
        lg = sb("lg", [P, 4, E1], scope=scope_f)
        lgd = sb("lgd", [P, 4, E1], scope=scope_f)
        gex = sb("gex", [P, 4, E1], scope=scope_f)
        ghot = sb("ghot", [P, 4, E1], scope=scope_f)
        gred = sb("gred", [P, 3, 4], scope=scope_f)
        cmp_gt = sb("cmp_gt", [P, 4, E1 * E1], scope=scope_f)
        cmp_eq = sb("cmp_eq", [P, 4, E1 * E1], scope=scope_f)
        g2 = sb("g2", [P, 4, 2 * E1], F32R, scope=scope_f)
        gT = sb("gT", [2 * E1, 2, BLK], F32R, scope=scope_f)
        scope_f.close()

        scope_c = ExitStack()
        KEYS = NT + NCTX
        key_row = sb("key_row", [P, KEYS], scope=scope_c)
        q32 = sb("q32", [P, 2, 512], scope=scope_c)
        k32 = sb("k32", [P, 3, 512], scope=scope_c)
        v32 = sb("v32", [P, 2, 3, 512], scope=scope_c)
        sq = sb("sq", [P, 512], scope=scope_c)
        ss = sb("ss", [P, 5, H1], scope=scope_c)
        rq = sb("rq", [P, 2, H1], scope=scope_c)
        qcT = sb("qcT", [P, 4, NT], scope=scope_c)
        kcT = sb("kcT", [P, 4, KEYS], scope=scope_c)
        sc = sb("sc", [P, 2, 4, KEYS], scope=scope_c)
        rs_qk = sb("rs_qk", [P, 3, 48], scope=scope_c)
        on1 = sb("on1", [P, 2, 2, P], scope=scope_c)
        smx = sb("smx", [P, 4, 4], scope=scope_c)
        smx2 = sb("smx2", [P, 4, 4], scope=scope_c)
        pcT = sb("pcT", [P, 3, 512], scope=scope_c)
        ocT = sb("ocT", [P, 4, NT], scope=scope_c)
        yn = sb("yn", [P, 2, P], scope=scope_c)
        qks = sb("qks", [P, 1], scope=scope_c)
        lno = sb("lno", [P, 2, P], scope=scope_c)
        latn = sb("latn", [P, 2, P], scope=scope_c)
        lat32 = sb("lat32", [P, NT], scope=scope_c)
        kv_hi, kv_lo = (sb(n, [P, 2, KEYS], F32R, scope=scope_c) for n in ("kv_hi", "kv_lo"))
        scope_c.close()

        x_loaded, small_loaded = sem("x_loaded"), sem("small_loaded")
        staged = [sem("staged_0"), sem("staged_1")]
        split, split_hi = sem("split"), sem("split_hi")
        late_loaded = sem("late_loaded")
        rw_ready = sem("rw_ready")
        gate_ready = sem("gate_ready")
        stored = sem("stored")
        dve_own = Chain(sem("dve_own"))
        a_k, a_kdone, a_ctxdup, a_xq, a_t, a_xqT, a_qv, a_q, a_v, a_kb, a_s, a_sm, a_exp, a_pt, a_pT, a_pv, a_on, \
            a_ot, a_oT, a_y, a_x = (sem(n) for n in (
                "a_k_products", "a_setup_read", "a_ctxdup", "a_xq", "a_xq_turned", "a_xqT", "a_qv_products", "a_q",
                "a_v", "a_kbd", "a_scores", "a_masked", "a_exp", "a_p_turned", "a_pT", "a_pv", "a_on", "a_o_turned",
                "a_oT", "a_y", "a_x"))
        f_xn, f_t, f_xhi, f_xlo, f_lg, f_lgd, f_ex, f_g2, f_gt, f_gT = (sem(n) for n in (
            "f_xn", "f_x_turned", "f_x_hi", "f_x_lo", "f_logits", "f_logits_read", "f_gate_exp", "f_gate",
            "f_gate_turned", "f_gT"))
        f_up, f_silu, f_h, f_hi, f_lo, f_down, f_G, f_gbc, f_yg, f_acc, f_at, f_x = (sem(n) for n in (
            "f_up", "f_silu", "f_h", "f_h_hi", "f_h_lo", "f_down", "f_gate_spread", "f_gate_bc", "f_yg",
            "f_acc", "f_acc_turned", "f_x"))

        ctx_loaded = sem("ctx_loaded")
        c_cn, c_ct, c_c32, c_chi, c_clo, c_setup = (sem(n) for n in (
            "c_ctx_rows", "c_ctx_turned", "c_ctx32", "c_ctx_hi", "c_ctx_lo", "c_setup"))
        c_xn, c_t, c_lat32, c_hi, c_lo, c_proj, c_qk, c_sq, c_ss, c_v, c_kn, c_qt, c_tev = (sem(n) for n in (
            "c_rows", "c_turned", "c_lat32", "c_kv_hi", "c_kv_lo", "c_projected", "c_qk_read", "c_squares", "c_sums",
            "c_values_read", "c_keys_normed", "c_qk_turned", "c_qk_turned_read"))
        c_s, c_sm, c_nb, c_exp, c_pt, c_pT0, c_pT1, c_pT2, c_pv, c_oT, c_y, c_yd, c_rq, c_on, c_ot = (sem(n) for n in (
            "c_scores", "c_masked", "c_bias", "c_exp", "c_p_turned", "c_pT0", "c_pT1", "c_pT2", "c_pv",
            "c_oT", "c_y", "c_y_read", "c_rq", "c_on", "c_o_turned"))
        TILE_ROWS = (P, P, NCTX)

        CHUNKS = (("q", 0), ("k", 0), ("k", 1), ("q", 2), ("k", 2), ("k", 3))

        def nothing():
            pass

        def n_from(n, first):
            return not isinstance(n, int) or n >= first

        ds = bass.ds

        def rsqrt_guess(dve, v, n, mul, add, least=None, buf=None):
            link, buf = linker(dve), rs if buf is None else buf
            a, y = buf[:, 0, 0:n], buf[:, 1, 0:n]
            if least is None:
                link(dve.tensor_scalar(a, v, mul, add, ALU.mult, ALU.add))
            else:
                link(dve.tensor_scalar(a, v, least, None, ALU.max))
            link(dve.tensor_scalar(y.bitcast(I32), a.bitcast(I32), 1, None, ALU.logical_shift_right))
            link(dve.tensor_scalar(y.bitcast(I32), y.bitcast(I32), -1.0, float(MAGIC), ALU.mult, ALU.add))

        def rsqrt_step(dve, n, buf=None):
            link, buf = linker(dve), rs if buf is None else buf
            a, y, s = buf[:, 0, 0:n], buf[:, 1, 0:n], buf[:, 2, 0:n]
            link(dve.scalar_tensor_tensor(out=s, in0=y, scalar=-0.5, in1=y, op0=ALU.mult, op1=ALU.mult))
            link(dve.tensor_tensor(s, s, a, ALU.mult))
            link(dve.scalar_tensor_tensor(out=y, in0=s, scalar=1.5, in1=y, op0=ALU.add, op1=ALU.mult))

        def rsqrt(dve, v, n, mul, add, least=None, buf=None):
            rsqrt_guess(dve, v, n, mul, add, least, buf)
            for _ in range(3):
                rsqrt_step(dve, n, buf)
            return (rs if buf is None else buf)[:, 1, 0:n]
        RSQRT_STEPS = 12

        def linker(dve):
            def link(ins):
                dve_own.k += 1
                ins.then_inc(dve_own.sem, 1)
                dve.wait_ge(dve_own.sem, dve_own.value())
            return link

        block = ctx.enter_context(nc.Block())

        @block.sync
        def _(sp):
            sp.dma_start(ctxr[:, :, :], ins["ctx"].rearrange("(t p) d -> p t d", p=P)).then_inc(ctx_loaded, 16)
            for dst, name in ((ctxT[:, :], "ctxT"), (wA[:, :, :], "wA"), (cst[:, :], "cst"), (rows[:, :], "rows"),
                              (cols[:, :], "cols"), (pad[:, :, :], "pad")):
                sp.dma_start(dst, ins[name]).then_inc(small_loaded, 16)
            rows_x = ins["x"].rearrange("(t p) d -> p t d", p=P)
            sp.dma_start(x[:, :, :], rows_x).then_inc(x_loaded, 16)
            for dst, name in ((kmask[:, :, :], "kmask"), (rw[:, :], "rw"), (wo1[:, :, :], "wo1"), (sel32[:, :], "sel")):
                sp.dma_start(dst, ins[name]).then_inc(late_loaded, 16)
            for n, (src, at, _, _, width) in enumerate(JOBS):
                if n >= 2:
                    sp.wait_ge(split, n - 1)
                sp.dma_start(stage[:, n % 2, 0:width], ins[src][:, at:at + width]).then_inc(staged[n % 2], 16)
            sp.wait_ge(f_x, FREE_X + 2 * NBLK)
            sp.dma_start(out.rearrange("(t p) d -> p t d", p=P), x[:, :, :]).then_inc(stored, 16)
            sp.wait_ge(stored, 16)
        SMALL, LATE = 6 * 16, 4 * 16

        @block.gpsimd
        def _(pool):
            def split_job(n):
                src, at, dst, to, width = JOBS[n]
                hi, lo = {"w": (w_hi, w_lo), "wa": (wa_hi, wa_lo)}[dst]
                st = stage[:, n % 2, 0:width]
                pool.wait_ge(staged[n % 2], 16 * (n // 2 + 1))
                pool.tensor_scalar(hi[:, to:to + width], st, 1.0, None, ALU.mult).then_inc(split_hi, 1)
                pool.wait_ge(split_hi, n + 1)
                pool.tensor_tensor(lo[:, to:to + width], st, hi[:, to:to + width].bitcast(F32),
                                   ALU.subtract).then_inc(split, 1)

            def add_experts(L):
                X = L.experts
                with pool.Fori(0, NBLK // 2) as i:
                    for k in range(2):
                        blk = i * 2 + k
                        for e in range(1, X):
                            pool.wait_ge(f_yg, FREE_YG + L.expert0 + blk * X + e + 1)
                            pool.wait_ge(f_acc, FREE_ACC + L.adds + blk * (X - 1) + e - 1)
                            pool.tensor_tensor(acc[:, k, :], acc[:, k, :], yg[:, e % 2, :], ALU.add).then_inc(f_acc, 1)

            for n in range(JOBS_C):
                split_job(n)
            add_experts(L0)
            pool.wait_ge(f_x, FREE_X + NBLK)
            for n in range(JOBS_C, len(JOBS)):
                split_job(n)
            add_experts(L1)

        @block.tensor
        def _(pe):
            def a_front(i):
                pe.wait_ge(a_xq, i + 1)
                pe.wait_ge(a_v, FREE_A + i)
                for b in range(2):
                    mm = pe.transpose(bank[0][:, b * P:(b + 1) * P], xq[:, b, :], eye)
                mm.then_inc(a_t, 1)
                pe.wait_ge(a_xqT, i + 1)
                qin = xqT[:, :, :].rearrange("p a b -> p (a b)")
                pe.matmul(bank[0][:, 256:384], wA[:, 0, :], qin, start=True, stop=True)
                pe.matmul(bank[0][:, 384:512], wA[:, 1, :], qin, start=True, stop=True)
                pe.wait_ge(a_ctxdup, i + 1)
                for b in range(2):
                    mm = pe.matmul(bank[0][:, b * P:(b + 1) * P], ctxdup[:, b, :, :].rearrange("p a b -> p (a b)"),
                                   wA[:, 4, :], start=True, stop=True)
                mm.then_inc(a_qv, 1)

            def a_scores(i):
                pe.wait_ge(a_q, i + 1)
                pe.wait_ge(a_sm, FREE_A + i)
                for b in range(2):
                    for g in range(4):
                        mm = pe.matmul(bank[1 + g][64 * b:64 * b + 64, 0:256], qT[32 * g:32 * g + 32, b, :],
                                       kbd[32 * g:32 * g + 32, b, :, :].rearrange("p a b -> p (a b)"),
                                       start=True, stop=True)
                mm.then_inc(a_s, 1)

            def a_body(i, last):
                if not last:
                    a_front(i + 1)
                pe.wait_ge(a_exp, i + 1)
                pe.wait_ge(a_pT, FREE_A + i)
                pe.wait_ge(a_x, FREE_A + i)
                for h in range(8):
                    mm = pe.transpose(bank[5 + h // 4][:, (h % 4) * P:(h % 4 + 1) * P],
                                      pr[:, 2 * h:2 * h + 2, :].rearrange("p a b -> p (a b)"), eye)
                mm.then_inc(a_pt, 1)
                pe.wait_ge(a_kb, i + 1)
                pe.wait_ge(a_pT, FREE_A + i + 1)
                pe.wait_ge(a_oT, FREE_A + i)
                for b in range(2):
                    for h in range(8):
                        mm = pe.matmul(bank[7][64 * b:64 * b + 64, 16 * h:16 * h + 16], pT[:, h, 64 * b:64 * b + 64],
                                       vbd[:, b, h, :], start=True, stop=True)
                mm.then_inc(a_pv, 1)
                if not last:
                    a_scores(i + 1)
                pe.wait_ge(a_on, i + 1)
                pe.transpose(bank[7][:, P:2 * P], on[:, :], eye).then_inc(a_ot, 1)
                pe.wait_ge(a_oT, FREE_A + i + 1)
                for t in range(4):
                    mm = pe.matmul(bank[5][:, t * P:(t + 1) * P], oT[:, t // 2, (t % 2) * P:(t % 2 + 1) * P],
                                   wA[:, 5, :], start=True, stop=True)
                mm.then_inc(a_y, 1)

            pe.wait_ge(small_loaded, SMALL)
            for half in range(2):
                cx = ctxT[:, half * 512:(half + 1) * 512]
                pe.matmul(bank[1 + 2 * half][:, :], wA[:, 2, :], cx, start=True, stop=True)
                mm = pe.matmul(bank[2 + 2 * half][:, :], wA[:, 3, :], cx, start=True, stop=True)
            mm.then_inc(a_k, 1)
            pe.wait_ge(a_kdone, 1)
            pe.matmul(bank[5][:, 0:NB], wA[:, 4, :], mctx[:, :], start=True, stop=True).then_inc(a_k, 1)
            for half in range(2):
                pe.wait_ge(c_cn, 1)
                for t in range(4):
                    mm = pe.transpose(bank[6 + half][:, t * P:(t + 1) * P], ctxr[:, 4 * half + t, :], eye)
                mm.then_inc(c_ct, 1)
            a_front(0)
            pe.wait_ge(c_chi, 2)
            pe.wait_ge(a_kdone, 2)
            a_scores(0)
            with pe.Fori(0, NB // 2 - 1) as i:
                a_body(i, False)
            a_body(NB // 2 - 1, True)

            def ffn(L):
                U, X, E = L.units, L.experts, L.E

                def x_turn(n, x_updates):
                    pe.wait_ge(f_xn, L.blocks + n + 1)
                    pe.wait_ge(f_x, FREE_X + L.blocks + x_updates)
                    for t in range(4):
                        mm = pe.transpose(bank[7][:, t * P:(t + 1) * P], xn[:, t, :], eye)
                    mm.then_inc(f_t, 1)

                def logits(n, k):
                    pe.wait_ge(f_xlo, L.blocks + n + 1)
                    for t in range(4):
                        o = t * 2 * E
                        pe.matmul(bank[7][:, o:o + 2 * E], xs_hi[:, k, t * P:(t + 1) * P], rw_r[:, L.rw0:L.rw0 + 2 * E],
                                  start=True, stop=False, skip_group_check=True)
                        mm = pe.matmul(bank[7][:, o:o + E], xs_lo[:, k, t * P:(t + 1) * P], rw_r[:, L.rw0:L.rw0 + E],
                                       start=False, stop=True, skip_group_check=True)
                    mm.then_inc(f_lg, 1)

                def gate_turn(n):
                    pe.wait_ge(f_g2, L.blocks + n + 1)
                    for t in range(4):
                        mm = pe.transpose(bank[7][0:2 * E, t * P:(t + 1) * P], g2[:, t, 0:2 * E].bitcast(F32), eye)
                    mm.then_inc(f_gt, 1)

                def acc_turn(n, k, gates_read):
                    pe.wait_ge(f_acc, FREE_ACC + L.adds + (n + 1) * (X - 1))
                    pe.wait_ge(f_gT, L.blocks + gates_read)
                    for t in range(4):
                        mm = pe.transpose(bank[7][:, t * P:(t + 1) * P], acc[:, k, t * P:(t + 1) * P], eye)
                    mm.then_inc(f_at, 1)

                def up(n, u, k):
                    e, c, width, c1, c2, _ = L.plan[u]
                    s = (k * U + u) % 2
                    pe.wait_ge(f_h, FREE_H + L.unit0 + n - 1)
                    for to, cc in ((bank[s], c1), (bank[2 + s], c2)):
                        for q, (wt, xt) in enumerate(((w_hi, xs_hi), (w_hi, xs_lo), (w_lo, xs_hi))):
                            mm = pe.matmul(to[0:width, :], wt[:, cc:cc + width], xt[:, k, :],
                                           start=(q == 0), stop=(q == 2))
                    mm.then_inc(f_up, 1)

                def down(n, u, k, m):
                    e, c, width, _, _, c3 = L.plan[u]
                    s = (k * U + u) % L.bufs
                    y = bank[4 + (k * X + e) % 2]
                    pe.wait_ge(f_lo, L.unit0 + n + 1)
                    if c == 0:
                        pe.wait_ge(f_yg, FREE_YG + L.expert0 + m - 1)
                    for q, (wt, ht) in enumerate(((w_hi, h_hi), (w_hi, h_lo), (w_lo, h_hi))):
                        mm = pe.matmul(y[:, :], wt[0:width, c3:c3 + P], ht[0:width, s, :],
                                       start=(c == 0 and q == 0), stop=(c == L.chunks - 1 and q == 2))
                    mm.then_inc(f_down, 1)

                def spread(n, e, k):
                    g = n * E + (e - L.gated0)
                    pe.wait_ge(f_gbc, L.gates + g)
                    if e == L.gated0:
                        pe.wait_ge(f_gT, L.blocks + n + 1)
                    at = (L.sel0 + e - L.gated0) * P
                    pe.matmul(bank[6][:, :], sel[0:2 * E, at:at + P], gT[0:2 * E, k, :], start=True,
                              stop=True).then_inc(f_G, 1)

                def slot(blk, u, k, more, after_one):
                    e, c, *_ = L.plan[u]
                    n = blk * U + u
                    up(n, u, k)
                    if c == 1 and e >= L.gated0:
                        spread(blk, e, k)
                    if u >= LAG:
                        down(n - LAG, u - LAG, k, blk * X + L.plan[u - LAG][0])
                    elif after_one:
                        down(n - LAG, U + u - LAG, 1 - k, (blk - 1) * X + L.plan[U + u - LAG][0])
                    if after_one and u == ACC_TURN:
                        acc_turn(blk - 1, 1 - k, blk + 1)
                    if more and u == X_TURN:
                        x_turn(blk + 1, blk)
                    if more and u == LOGITS:
                        logits(blk + 1, 1 - k)
                    if more and u == GATE_TURN:
                        gate_turn(blk + 1)
                    if L is L0 and not more and k == 1 and u == X_TURN:
                        pe.wait_ge(f_x, FREE_X + NBLK - 1)
                        c_turn(0)

                if L is L1:
                    pe.wait_ge(c_yd, NB)
                x_turn(0, 0)
                logits(0, 0)
                gate_turn(0)
                pe.wait_ge(split, L.jobs)
                for u in range(ROT):
                    slot(0, u, 0, True, False)
                with pe.Fori(0, NBLK // 2 - 1) as i:
                    for j in range(ROT, 2 * U + ROT):
                        slot(2 * i + j // U, j % U, j // U % 2, True, True)
                for j in range(ROT, 2 * U):
                    slot(NBLK - 2 + j // U, j % U, j // U % 2, j < U, True)
                for u in range(U - LAG, U):
                    down((NBLK - 1) * U + u, u, 1, (NBLK - 1) * X + L.plan[u][0])
                if L is L0:
                    pe.wait_ge(c_lat32, 1)
                acc_turn(NBLK - 1, 1, NBLK)

            def c_turn(n):
                pe.wait_ge(c_xn, n + 1)
                if n_from(n, 2):
                    pe.wait_ge(c_oT, 4 * n - 6)
                for t in range(2):
                    mm = pe.transpose(bank[7][:, t * P:(t + 1) * P], latn[:, t, :], eye)
                mm.then_inc(c_t, 1)

            def c_project(n, par, j):
                if j == 0:
                    pe.wait_ge(c_lo, n + 1)
                    if n_from(n, 1):
                        pe.wait_ge(c_v, 3 * n - 1)
                elif j == 1:
                    if n_from(n, 1):
                        pe.wait_ge(c_v, 3 * n)
                elif j < 5:
                    pe.wait_ge(c_qk, 5 * n + j - 1)
                elif j < 7:
                    pe.wait_ge(c_tev, 6 * n + 11 - j)
                else:
                    pe.wait_ge(c_v, 3 * n + 1)
                t, w0 = (j, 0) if j < 2 else (j - 2, 512) if j < 5 else (j - 5, 1024)
                r = TILE_ROWS[t]
                hi, lo = kv_hi[:, par, t * P:t * P + r], kv_lo[:, par, t * P:t * P + r]
                for q, (xt, wt) in enumerate(((hi, wa_hi), (hi, wa_lo), (lo, wa_hi))):
                    mm = pe.matmul(bank[5 + j % 2][0:r, :], xt, wt[:, w0:w0 + 512], start=(q == 0), stop=(q == 2))
                mm.then_inc(c_proj, 1)

            def c_turn_qk(n, f):
                to = bank[5 + f % 2]
                if f < 2:
                    pe.wait_ge(c_qk, 5 * n + 5)
                else:
                    pe.wait_ge(c_tev, 6 * n + f - 1)
                kind, c = CHUNKS[f]
                if kind == "q":
                    for k in (0, 1):
                        for t in range(2):
                            at = (c + k) * P
                            mm = pe.transpose(to[:, k * NT + t * P:k * NT + (t + 1) * P], q32[:, t, at:at + P], eye)
                else:
                    pe.wait_ge(c_kn, n + 1)
                    for t in range(3):
                        r = TILE_ROWS[t]
                        mm = pe.transpose(to[:, t * P:t * P + r], k32[0:r, t, c * P:(c + 1) * P], eye[0:r, 0:r])
                mm.then_inc(c_qt, 1)

            def c_scores(n, g, half):
                pe.wait_ge(c_tev, 6 * n + (2, 3, 5, 6)[g])
                for t in range(2):
                    z = 4 * g + 2 * half + t
                    if n_from(n, 1) or z >= 2:
                        pe.wait_ge(c_sm, 16 * n + z - 1)
                    pe.matmul(bank[z % 2][:, 0:KEYS], qcT[64 * half:64 * half + 64, g, t * P:(t + 1) * P],
                              kcT[64 * half:64 * half + 64, g, :], start=True, stop=True).then_inc(c_s, 1)

            def c_turn_p(n, g, kt):
                m = 4 * n + g
                if kt == 0:
                    pe.wait_ge(c_exp, 2 * m + 2)
                if kt < 2 and (n_from(n, 1) or m > 0):
                    pe.wait_ge((c_pT1, c_pT2)[kt], m)
                r = TILE_ROWS[kt]
                for it in range(4):
                    if kt == 1 and it == 3:
                        pe.wait_ge(c_pT0, m + 1)
                    mm = pe.transpose(bank[2 + (3 * g + kt) % 2][0:r, it * P:(it + 1) * P],
                                      sc[:, g % 2, it, kt * P:kt * P + r], eye)
                mm.then_inc(c_pt, 1)

            def c_values(n, par, g):
                m = 4 * n + g
                if n_from(n, 1) or m > 0:
                    pe.wait_ge(c_on, m)
                pe.wait_ge(c_v, 3 * n + 3)
                pe.wait_ge(c_pT1, m + 1)
                pe.wait_ge(c_pT2, m + 1)
                for it in range(4):
                    h = 2 * g + it // 2
                    for kt in range(3):
                        r = TILE_ROWS[kt]
                        mm = pe.matmul(bank[4][:, it * C1:(it + 1) * C1], pcT[0:r, kt, it * P:(it + 1) * P],
                                       v32[0:r, par, kt, h * C1:(h + 1) * C1], start=(kt == 0), stop=(kt == 2),
                                       skip_group_check=True)
                mm.then_inc(c_pv, 1)

            def c_turn_o(n, g, more2=True):
                m = 4 * n + g
                pe.wait_ge(c_on, m + 1)
                if n_from(n, 1) or m > 0:
                    pe.wait_ge(c_oT, m)
                if g == 0 and n_from(n, 1):
                    pe.wait_ge(c_yd, n)
                if g == 2:
                    pe.wait_ge(c_lat32, n + 3 if more2 else NB)
                for t in range(2):
                    mm = pe.transpose(bank[7][:, t * P:(t + 1) * P], on1[:, g % 2, t, :], eye)
                mm.then_inc(c_ot, 1)

            def c_out(n):
                pe.wait_ge(c_oT, 4 * n + 4)
                for t in range(2):
                    for g in range(4):
                        mm = pe.matmul(bank[7][:, t * P:(t + 1) * P], ocT[:, g, t * P:(t + 1) * P], wo1[:, g, :],
                                       start=(g == 0), stop=(g == 3))
                mm.then_inc(c_y, 1)

            def c_slot(n, par, g, first, second, ahead):
                if ahead:
                    c_scores(*ahead, 0)
                first()
                for kt in range(3):
                    c_turn_p(n, g, kt)
                if ahead:
                    c_scores(*ahead, 1)
                second()
                c_values(n, par, g)

            def c_slot0(n, par, more, first_one):
                def first():
                    c_project(n, par, 7)
                    if more:
                        c_project(n + 1, 1 - par, 0)

                def second():
                    if more:
                        c_project(n + 1, 1 - par, 1)
                        c_project(n + 1, 1 - par, 2)
                    if not first_one:
                        c_turn_o(n - 1, 3)
                c_slot(n, par, 0, first, second, (n, 1))

            def c_body(n, par, more, more2):
                def first1():
                    if more:
                        c_project(n + 1, 1 - par, 3)
                        c_project(n + 1, 1 - par, 4)
                    if n_from(n, 1):
                        c_out(n - 1)
                c_slot(n, par, 1, first1, lambda: c_turn_o(n, 0), (n, 2))

                def first2():
                    if more:
                        c_turn_qk(n + 1, 0)

                def second2():
                    if more:
                        c_turn_qk(n + 1, 1)
                        c_turn_qk(n + 1, 2)
                    c_turn_o(n, 1)
                c_slot(n, par, 2, first2, second2, (n, 3))

                def first3():
                    if more:
                        for f in range(3, 6):
                            c_turn_qk(n + 1, f)

                def second3():
                    if more2:
                        c_turn(n + 2)
                    if more:
                        c_project(n + 1, 1 - par, 5)
                        c_project(n + 1, 1 - par, 6)
                    c_turn_o(n, 2, more2)
                c_slot(n, par, 3, first3, second3, (n + 1, 0) if more else None)
                if more:
                    c_slot0(n + 1, 1 - par, more2, False)
                else:
                    c_turn_o(n, 3)
                    c_out(n)

            def pass_c():
                pe.wait_ge(split, JOBS_C)
                for j in range(5):
                    c_project(0, 0, j)
                for f in range(6):
                    c_turn_qk(0, f)
                c_project(0, 0, 5)
                c_project(0, 0, 6)
                c_turn(1)
                c_scores(0, 0, 0)
                c_scores(0, 0, 1)
                c_slot0(0, 0, True, True)
                c_body(0, 0, True, True)
                with pe.Fori(0, (NB - 4) // 2) as i:
                    c_body(2 * i + 1, 1, True, True)
                    c_body(2 * i + 2, 0, True, True)
                c_body(NB - 3, 1, True, True)
                c_body(NB - 2, 0, True, False)
                c_body(NB - 1, 1, False, False)

            pe.wait_ge(rw_ready, 2)
            ffn(L0)
            pass_c()
            ffn(L1)

        @block.scalar
        def _(act):
            act.wait_ge(small_loaded, SMALL)
            act.activation(tg[:, :], row("g"), ACT.Tanh).then_inc(gate_ready, 1)

            def a_ctxdup_copy(i):
                act.wait_ge(a_qv, FREE_A + i)
                src = ctxT[:, ds(i * P, P)].rearrange("p (b j) -> p b j", b=2)
                for d in range(2):
                    ins_ = act.copy(ctxdup[:, :, d, :], src)
                ins_.then_inc(a_ctxdup, 1)

            def a_xqT_copy(i):
                act.wait_ge(a_t, FREE_A + i + 1)
                act.copy(xqT[:, :, :], bank[0][:, 0:256].rearrange("p (b j) -> p b j", b=2)[:, :, 64:128])\
                   .then_inc(a_xqT, 1)

            def a_body(i, last):
                if not last:
                    a_ctxdup_copy(i + 1)
                    a_xqT_copy(i + 1)
                act.wait_ge(a_sm, FREE_A + i + 1)
                act.wait_ge(a_pt, FREE_A + i)
                act.activation(pr[:, :, :], sm[:, :, :], ACT.Exp).then_inc(a_exp, 1)
                act.wait_ge(a_pt, FREE_A + i + 1)
                act.wait_ge(a_pv, FREE_A + i)
                act.copy(pT[:, 0:4, :].rearrange("p a b -> p (a b)"), bank[5][:, :])
                act.copy(pT[:, 4:8, :].rearrange("p a b -> p (a b)"), bank[6][:, :]).then_inc(a_pT, 1)
                act.wait_ge(a_ot, i + 1)
                act.copy(oT[:, :, 192:256], bank[7][:, P:2 * P].rearrange("p (b j) -> p b j", b=2)).then_inc(a_oT, 1)

            a_ctxdup_copy(0)
            for half in range(2):
                part = slice(half * 512, (half + 1) * 512)
                act.wait_ge(c_ct, half + 1)
                act.activation(ctx32[:, part], bank[6 + half][:, :], ACT.Identity, scale=col("ln_x_w"),
                               bias=col("ln_x_b")).then_inc(c_c32, 1)
                act.wait_ge(c_c32, half + 1)
                act.copy(ctx_hi[:, part], ctx32[:, part]).then_inc(c_chi, 1)
            a_xqT_copy(0)
            act.wait_ge(late_loaded, LATE)
            act.copy(sel[:, :], sel32[:, :]).then_inc(rw_ready, 1)
            with act.Fori(0, NB // 2 - 1) as i:
                a_body(i, False)
            a_body(NB // 2 - 1, True)

            def ffn(L):
                U, X, E = L.units, L.experts, L.E

                def x_hi(n, k):
                    act.wait_ge(f_t, L.blocks + n + 1)
                    act.copy(xs_hi[:, k, :], bank[7][:, :]).then_inc(f_xhi, 1)

                def gate_exp(n):
                    act.wait_ge(f_lgd, L.blocks + n + 1)
                    act.activation(gex[:, :, 0:E], lgd[:, :, 0:E], ACT.Exp).then_inc(f_ex, 1)

                def gates_in(n, k):
                    act.wait_ge(f_gt, L.blocks + n + 1)
                    act.copy(gT[0:2 * E, k, :], bank[7][0:2 * E, :]).then_inc(f_gT, 1)

                def silu(n, u, k):
                    width, s = L.plan[u][2], (k * U + u) % 2
                    act.wait_ge(f_up, L.unit0 + n + 1)
                    act.activation(act_t[0:width, s, :], bank[s][0:width, :], ACT.Silu).then_inc(f_silu, 1)

                def h_high(n, u, k):
                    width = L.plan[u][2]
                    to = h_hi[0:width, (k * U + u) % L.bufs, :]
                    act.wait_ge(f_h, FREE_H + L.unit0 + n + 1)
                    act.wait_ge(f_down, FREE_DOWN + L.unit0 + n + 1 - L.bufs)
                    act.copy(to, h32[0:width, (k * U + u) % L.bufs32, :]).then_inc(f_hi, 1)

                def gate_bc(n, e, k):
                    g = n * E + (e - L.gated0)
                    act.wait_ge(f_G, L.gates + g + 1)
                    m = n * X + e
                    act.wait_ge(f_yg, FREE_YG + L.expert0 + m - 1)
                    act.copy(g_bc[:, (k * X + e) % 2, :], bank[6][:, :]).then_inc(f_gbc, 1)

                def slot(blk, u, k, more, after_one):
                    e, c, *_ = L.plan[u]
                    n = blk * U + u
                    silu(n, u, k)
                    if u >= 1:
                        h_high(n - 1, u - 1, k)
                    elif after_one:
                        h_high(n - 1, U - 1, 1 - k)
                    if e >= L.gated0 and c == L.chunks - 1:
                        gate_bc(blk, e, k)
                    if more and u == X_HI:
                        x_hi(blk + 1, 1 - k)
                    if more and u == GATE_EXP:
                        gate_exp(blk + 1)
                    if more and u == GATES_IN:
                        gates_in(blk + 1, 1 - k)
                    if L is L0 and not more and k == 1 and u == X_HI:
                        c_inputs(0, 0)

                x_hi(0, 0)
                gate_exp(0)
                gates_in(0, 0)
                for u in range(ROT):
                    slot(0, u, 0, True, False)
                with act.Fori(0, NBLK // 2 - 1) as i:
                    for j in range(ROT, 2 * U + ROT):
                        slot(2 * i + j // U, j % U, j // U % 2, True, True)
                for j in range(ROT, 2 * U):
                    slot(NBLK - 2 + j // U, j % U, j // U % 2, j < U, True)
                h_high(NBLK * U - 1, U - 1, 1)

            def c_inputs(n, par):
                act.wait_ge(c_t, n + 1)
                act.activation(lat32[:, :], bank[7][:, 0:NT], ACT.Identity, scale=col("ln_l_w"),
                               bias=col("ln_l_b")).then_inc(c_lat32, 1)
                act.wait_ge(c_lat32, n + 1)
                if n_from(n, 2):
                    act.wait_ge(c_proj, 8 * n - 8)
                act.copy(kv_hi[:, par, 0:NT], lat32[:, :])
                act.copy(kv_hi[:, par, NT:KEYS], ctx_hi[:, ds(n * NCTX, NCTX)].bitcast(F32)).then_inc(c_hi, 1)

            def c_qk_in(n, j):
                r = TILE_ROWS[j if j < 2 else j - 2]
                to = q32[0:r, j, :] if j < 2 else k32[0:r, j - 2, :]
                act.wait_ge(c_proj, 8 * n + j + 1)
                act.copy(to, bank[5 + j % 2][0:r, :]).then_inc(c_qk, 1)
                if n_from(n, 1) or j > 0:
                    act.wait_ge(c_ss, 5 * n + j)
                act.wait_ge(c_qk, 5 * n + j + 1)
                act.activation(sq[0:r, :], to, ACT.Square).then_inc(c_sq, 1)

            def c_turned_in(n, f):
                act.wait_ge(c_qt, 6 * n + f + 1)
                kind, c = CHUNKS[f]
                if kind == "q":
                    act.copy(qcT[:, c:c + 2, :].rearrange("p a b -> p (a b)"), bank[5 + f % 2][:, :])\
                       .then_inc(c_tev, 1)
                else:
                    act.activation(kcT[:, c, :], bank[5 + f % 2][:, 0:KEYS], ACT.Copy, scale=qks[:, 0:1])\
                       .then_inc(c_tev, 1)

            def c_exps(n, g, half):
                m = 4 * n + g
                act.wait_ge(c_nb, 2 * m + half + 1)
                small = smx if g % 2 == 0 else smx2
                h = 2 * g + half
                for it in (2 * half, 2 * half + 1):
                    s_ = sc[:, g % 2, it, :]
                    ins_ = act.activation(s_, s_, ACT.Exp, scale=rq[:, it % 2, h:h + 1], bias=small[:, 1, it:it + 1],
                                          accum_out=small[:, 2, it:it + 1])
                ins_.then_inc(c_exp, 1)

            def c_p_in(n, g):
                m = 4 * n + g
                if n_from(n, 1) or m > 0:
                    act.wait_ge(c_pv, m)
                act.wait_ge(c_pt, 3 * m + 1)
                act.copy(pcT[:, 0, :], bank[2 + (3 * g) % 2][:, :]).then_inc(c_pT0, 1)
                act.wait_ge(c_pt, 3 * m + 3)
                act.copy(pcT[0:NCTX, 2, :], bank[2 + (3 * g + 2) % 2][0:NCTX, :]).then_inc(c_pT2, 1)

            def c_o_in(n, g):
                act.wait_ge(c_ot, 4 * n + g + 1)
                act.copy(ocT[:, g, :], bank[7][:, 0:NT]).then_inc(c_oT, 1)

            def c_slot(n, g, before, first, after, ahead):
                before()
                first()
                c_p_in(n, g)
                if ahead:
                    c_exps(*ahead, 0)
                after()
                if ahead:
                    c_exps(*ahead, 1)

            def c_slot0(n, more, first_one):
                def after():
                    if more:
                        c_qk_in(n + 1, 0)
                c_slot(n, 0, nothing, nothing, after, (n, 1))
                if more:
                    c_qk_in(n + 1, 1)
                    c_qk_in(n + 1, 2)
                if not first_one:
                    c_o_in(n - 1, 3)

            def c_body(n, par, more, more2):
                def after1():
                    if more:
                        c_qk_in(n + 1, 3)
                        c_qk_in(n + 1, 4)

                def turned(*chunks):
                    def step():
                        if more:
                            for f in chunks:
                                c_turned_in(n + 1, f)
                    return step
                c_slot(n, 1, nothing, after1, nothing, (n, 2))
                c_o_in(n, 0)
                c_slot(n, 2, nothing, turned(0), nothing, (n, 3))
                turned(1, 2)()
                c_o_in(n, 1)
                c_slot(n, 3, turned(3, 4), turned(5), lambda: c_inputs(n + 2, par) if more2 else None,
                       (n + 1, 0) if more else None)
                c_o_in(n, 2)
                if more:
                    c_slot0(n + 1, more2, False)
                else:
                    c_o_in(n, 3)

            def pass_c():
                for j in range(5):
                    c_qk_in(0, j)
                act.wait_ge(c_setup, 1)
                for f in range(6):
                    c_turned_in(0, f)
                c_inputs(1, 1)
                c_exps(0, 0, 0)
                c_exps(0, 0, 1)
                c_slot0(0, True, True)
                c_body(0, 0, True, True)
                with act.Fori(0, (NB - 4) // 2) as i:
                    c_body(2 * i + 1, 1, True, True)
                    c_body(2 * i + 2, 0, True, True)
                c_body(NB - 3, 1, True, True)
                c_body(NB - 2, 0, True, False)
                c_body(NB - 1, 1, False, False)

            ffn(L0)
            pass_c()
            ffn(L1)

        @block.vector
        def _(dve):
            link = linker(dve)

            def waited(it=0):
                dve.memset(hold[:, it:it + 1], 0.0)

            def a_root():
                for b in range(NB):
                    ins_ = dve.bn_stats(q_stat[:, b, :], x[:, 2 * b + 1, :])
                link(ins_)
                for b in range(NB):
                    ins_ = dve.bn_aggr(q_mv[:, b, :], q_stat[:, b, :])
                link(ins_)
                rsqrt(dve, q_mv[:, :, 1], NB, 1.0, LN_EPS, buf=q_rs)

            def a_rows(i):
                dve.wait_ge(a_t, FREE_A + i)
                for b in range(2):
                    at = i * 2 + b
                    ins_ = dve.tensor_scalar(xq[:, b, :], x[:, ds(at * 2 + 1, 1), :].rearrange("p a d -> p (a d)"),
                                             q_mv[:, ds(at, 1), 0:1].rearrange("p a b -> p (a b)"),
                                             q_rs[:, 1, ds(at, 1)], ALU.subtract, ALU.mult)
                ins_.then_inc(a_xq, 1)

            def wide(ap, n):
                return ap.unsqueeze(1).to_broadcast([P, n, ap.shape[1]])

            def a_operands(i):
                dve.wait_ge(a_qv, FREE_A + i + 1)
                v3 = lambda a, b: bank[0][:, a:b].rearrange("p (b j) -> p b j", b=2)
                dve.scalar_tensor_tensor(out=qr1[:, :, :], in0=v3(256, 384), scalar=col("bq"), in1=wide(C("cos_q"), 2),
                                         op0=ALU.add, op1=ALU.mult)
                link(dve.scalar_tensor_tensor(out=qr2[:, :, :], in0=v3(384, 512), scalar=col("bq_swap"),
                                              in1=wide(C("sin_q"), 2), op0=ALU.add, op1=ALU.mult))
                dve.wait_ge(a_s, FREE_A + i)
                dve.tensor_tensor(qT[:, :, :], qr1[:, :, :], qr2[:, :, :], ALU.add)
                ksrc = krope[:, ds(i * P, P)].rearrange("p (b j) -> p b j", b=2)
                for h in range(4):
                    dve.tensor_scalar(kbd[:, :, h, :], ksrc, C("head_of")[:, h:h + 1], None, ALU.mult)
                vt = vtmp[:, :].rearrange("p (b c) -> p b c", b=2)
                ins_ = dve.tensor_tensor(vt, v3(0, 256), wide(row("bv"), 2), ALU.add)
                ins_.then_inc(a_v, 1)
                dve.wait_ge(a_v, FREE_A + i + 1)
                dve.memset(hold[:, 31:32], 0.0).then_inc(a_q, 1)

            def a_vbd(i):
                dve.tensor_tensor(vbd[:, :, :, :].rearrange("p b h c -> p (b h) c"),
                                  vtmp[:, :].rearrange("p (h c) -> p h c", c=16), wide(C("vhalf"), 16),
                                  ALU.mult).then_inc(a_kb, 1)

            def a_add(i):
                dve.wait_ge(a_y, FREE_A + i + 1)
                link(dve.tensor_tensor(ytmp[:, :, :], bank[5][:, :].rearrange("p (t d) -> p t d", t=4),
                                       wide(row("bo"), 4), ALU.add))
                xs = x[:, ds(i * 4, 4), :]
                dve.scalar_tensor_tensor(out=xs, in0=ytmp[:, :, :], scalar=tg[:, 0:1], in1=xs,
                                         op0=ALU.mult, op1=ALU.add).then_inc(a_x, 1)

            def a_body(i, first, last, rows_too=True):
                dve.wait_ge(a_s, FREE_A + i + 1)
                for g in range(4):
                    ins_ = dve.tensor_tensor(sm[:, 4 * g:4 * g + 4, :],
                                             bank[1 + g][:, 0:256].rearrange("p (h j) -> p h j", h=4),
                                             mneg[:, ds(i, 1), :].to_broadcast([P, 4, NCTX]), ALU.add)
                link(ins_)
                link(dve.tensor_reduce(sred[:, 0, :], sm[:, :, :], AX.X, ALU.max))
                dve.tensor_tensor(sm[:, :, :], sm[:, :, :], sred[:, 0, :].unsqueeze(2).to_broadcast([P, H0, NCTX]),
                                  ALU.subtract).then_inc(a_sm, 1)
                if not first:
                    a_add(i - 1)
                if not last:
                    a_operands(i + 1)
                dve.wait_ge(a_exp, i + 1)
                link(dve.tensor_reduce(sred[:, 1, :], pr[:, :, :], AX.X, ALU.add))
                link(dve.reciprocal(sred[:, 2, :], sred[:, 1, :]))
                if not last and rows_too:
                    a_rows(i + 2)
                if last:
                    first_rows()
                dve.wait_ge(a_y, FREE_A + i)
                for b in range(2):
                    dve.tensor_copy(oT[:, b, 0:192], omT[:, ds(i * 2 + b, 1)].to_broadcast([P, 192]))
                dve.wait_ge(a_pv, FREE_A + i + 1)
                dve.tensor_tensor(on[:, :].rearrange("p (h c) -> p h c", h=H0),
                                  bank[7][:, 0:P].rearrange("p (h c) -> p h c", h=H0),
                                  sred[:, 2, :].unsqueeze(2).to_broadcast([P, H0, C0]), ALU.mult).then_inc(a_on, 1)
                if not last:
                    a_vbd(i + 1)

            def stats(n):
                for t in range(4):
                    ins_ = dve.bn_stats(stat[:, t, :], x[:, ds(n * 4 + t, 1), :].rearrange("p a d -> p (a d)"))
                link(ins_)
                waited()
                for t in range(4):
                    ins_ = dve.bn_aggr(mv[:, t, :], stat[:, t, :])
                link(ins_)

            def rows_in(n):
                r = rs[:, 1, 0:4]
                for t in range(4):
                    ins_ = dve.tensor_scalar(xn[:, t, :], x[:, ds(n * 4 + t, 1), :].rearrange("p a d -> p (a d)"),
                                             mv[:, t, 0:1], r[:, t:t + 1], ALU.subtract, ALU.mult)
                ins_.then_inc(f_xn, 1)

            def first_rows():
                stats(0)
                rsqrt(dve, mv[:, :, 1], 4, 1.0, LN_EPS)
                rows_in(0)

            free = [(f_h, FREE_H), (f_down, FREE_DOWN), (f_yg, FREE_YG), (f_x, FREE_X), (f_acc, FREE_ACC)]
            free += [(what, FREE_A) for what in (a_v, a_sm, a_pT, a_x, a_oT, a_qv, a_pt, a_pv, a_t, a_s, a_y)]
            for k, (what, count) in enumerate(free):
                dve.memset(hold[:, 4 + k:5 + k], 0.0).then_inc(what, count)
            dve_own.start(0, 0)
            dve.wait_ge(ctx_loaded, 16)
            for t in range(NB // 2):
                ins_ = dve.bn_stats(ctx_stat[:, t, :], ctxr[:, t, :])
            link(ins_)
            for t in range(NB // 2):
                ins_ = dve.bn_aggr(ctx_mv[:, t, :], ctx_stat[:, t, :])
            link(ins_)
            r = rsqrt(dve, ctx_mv[:, :, 1], NB // 2, 1.0, LN_EPS)
            for t in range(NB // 2):
                ins_ = dve.tensor_scalar(ctxr[:, t, :], ctxr[:, t, :], ctx_mv[:, t, 0:1], r[:, t:t + 1],
                                         ALU.subtract, ALU.mult)
            ins_.then_inc(c_cn, 1)
            dve.wait_ge(c_cn, 1)
            dve.wait_ge(small_loaded, SMALL)
            dve.tensor_reduce(mctx[:, :], ctxT[:, :].rearrange("p (b j) -> p b j", j=NCTX), AX.X, ALU.add)\
               .then_inc(a_kdone, 1)
            link(dve.tensor_tensor(mneg[:, :, :], pad[:, :, :], wide(C("barred"), NB // 2), ALU.max))
            link(dve.tensor_scalar(mneg[:, :, :], mneg[:, :, :], NEG, None, ALU.mult))
            dve.wait_ge(x_loaded, 16)
            a_root()
            a_rows(0)
            dve.wait_ge(a_k, 1)
            for half in range(2):
                kr = krope[:, half * 512:(half + 1) * 512].rearrange("p (b j) -> p b j", j=NCTX)
                kt = ktmp[:, :].rearrange("p (b j) -> p b j", j=NCTX)
                b3 = lambda z: bank[z][:, :].rearrange("p (b j) -> p b j", j=NCTX)
                dve.scalar_tensor_tensor(out=kr, in0=b3(1 + 2 * half), scalar=col("bk"), in1=wide(C("cos_k"), 8),
                                         op0=ALU.add, op1=ALU.mult)
                link(dve.scalar_tensor_tensor(out=kt, in0=b3(2 + 2 * half), scalar=col("bk_swap"),
                                              in1=wide(C("sin_k"), 8), op0=ALU.add, op1=ALU.mult))
                link(dve.tensor_tensor(kr, kr, kt, ALU.add))
            dve.wait_ge(a_k, 2)
            link(dve.tensor_scalar(omT[:, :], bank[5][:, 0:NB], 1.0 / NCTX, col("bv"), ALU.mult, ALU.add))
            dve.engine_nop().then_inc(a_kdone, 1)
            dve.wait_ge(gate_ready, 1)
            a_rows(1)
            a_operands(0)
            a_vbd(0)
            for half in range(2):
                dve.wait_ge(c_chi, half + 1)
                a, b = half * 512, (half + 1) * 512
                dve.tensor_tensor(ctx_lo[:, a:b], ctx32[:, a:b], ctx_hi[:, a:b].bitcast(F32), ALU.subtract)\
                   .then_inc(c_clo, 1)
            dve_own.settle()
            steps = 2 + 2 + 1 + 1
            a_body(0, True, False)
            dve_own.settle()
            with dve.Fori(0, NB // 2 - 3) as i:
                dve_own.start(i, steps)
                a_body(i + 1, False, False)
                dve_own.end_body()
            dve_own.end(NB // 2 - 3)
            dve_own.start(0, 0)
            a_body(NB // 2 - 2, False, False, False)
            a_body(NB // 2 - 1, False, True)
            a_add(NB // 2 - 1)
            dve.wait_ge(late_loaded, LATE)
            for r0, c0, n in ((0, 0, E0), (2 * E0, E0, E1)):
                ins_ = dve.tensor_copy(rw_r[:, r0:r0 + n], rw[:, c0:c0 + n])
            link(ins_)
            for r0, c0, n in ((0, 0, E0), (2 * E0, E0, E1)):
                ins_ = dve.tensor_tensor(rw_r[:, r0 + n:r0 + 2 * n], rw[:, c0:c0 + n],
                                         rw_r[:, r0:r0 + n].bitcast(F32), ALU.subtract)
            ins_.then_inc(rw_ready, 1)
            dve_own.settle()

            def ffn(L):
                U, X, E = L.units, L.experts, L.E

                def x_lo(n, k):
                    dve.wait_ge(f_xhi, L.blocks + n + 1)
                    dve.tensor_tensor(xs_lo[:, k, :], bank[7][:, :], xs_hi[:, k, :].bitcast(F32),
                                      ALU.subtract).then_inc(f_xlo, 1)

                def logits_in(n):
                    dve.wait_ge(f_lg, L.blocks + n + 1)
                    two = bank[7][:, 0:8 * E].rearrange("p (t e) -> p t e", t=4)
                    l, d = lg[:, :, 0:E], lgd[:, :, 0:E]
                    link(dve.tensor_tensor(l, two[:, :, E:2 * E], wide(row(L.bias), 4), ALU.add))
                    link(dve.tensor_tensor(l, two[:, :, 0:E], l, ALU.add))
                    link(dve.tensor_reduce(gred[:, 0, :], l, AX.X, ALU.max))
                    dve.tensor_tensor(d, l, gred[:, 0, :].unsqueeze(2).to_broadcast([P, 4, E]), ALU.subtract)\
                       .then_inc(f_lgd, 1)

                def rank(n):
                    l = lg[:, :, 0:E]
                    gt = cmp_gt[:, :, 0:E * E].rearrange("p t (a b) -> p t a b", a=E)
                    eq = cmp_eq[:, :, 0:E * E].rearrange("p t (a b) -> p t a b", a=E)
                    other = l.unsqueeze(2).to_broadcast([P, 4, E, E])
                    own = l.unsqueeze(3).to_broadcast([P, 4, E, E])
                    dve.tensor_tensor(gt, other, own, ALU.is_gt)
                    link(dve.tensor_tensor(eq, other, own, ALU.is_equal))
                    link(dve.tensor_tensor(cmp_eq[:, :, 0:E * E], cmp_eq[:, :, 0:E * E], wide(C(L.tri), 4), ALU.mult))
                    link(dve.tensor_tensor(gt, gt, eq, ALU.add))
                    hot = ghot[:, :, 0:E]
                    link(dve.tensor_reduce(hot, gt, AX.X, ALU.add))
                    link(dve.tensor_scalar(hot, hot, float(L.K), None, ALU.is_lt))

                def weights(n):
                    hot = ghot[:, :, 0:E]
                    dve.wait_ge(f_ex, L.blocks + n + 1)
                    link(dve.tensor_tensor(hot, hot, gex[:, :, 0:E], ALU.mult))
                    link(dve.tensor_reduce(gred[:, 1, :], hot, AX.X, ALU.add))
                    link(dve.reciprocal(gred[:, 2, :], gred[:, 1, :]))
                    link(dve.tensor_scalar(gred[:, 2, :], gred[:, 2, :], tg[:, L.g:L.g + 1], None, ALU.mult))
                    link(dve.tensor_tensor(hot, hot, gred[:, 2, :].unsqueeze(2).to_broadcast([P, 4, E]), ALU.mult))
                    link(dve.tensor_copy(g2[:, :, 0:E], hot))
                    dve.tensor_tensor(g2[:, :, E:2 * E], hot, g2[:, :, 0:E].bitcast(F32), ALU.subtract)\
                       .then_inc(f_g2, 1)
                PREP = 2 + RSQRT_STEPS + 3 + 11

                def hidden(n, u, k):
                    width, s = L.plan[u][2], (k * U + u) % 2
                    dve.wait_ge(f_silu, L.unit0 + n + 1)
                    dve.tensor_tensor(h32[0:width, (k * U + u) % L.bufs32, :], act_t[0:width, s, :],
                                      bank[2 + s][0:width, :], ALU.mult).then_inc(f_h, 1)

                def h_low(n, u, k):
                    width, s, b = L.plan[u][2], (k * U + u) % L.bufs32, (k * U + u) % L.bufs
                    dve.wait_ge(f_hi, L.unit0 + n + 1)
                    dve.tensor_tensor(h_lo[0:width, b, :], h32[0:width, s, :], h_hi[0:width, b, :].bitcast(F32),
                                      ALU.subtract).then_inc(f_lo, 1)

                def weigh_expert(blk, e, k):
                    m = blk * X + e
                    dve.wait_ge(f_down, FREE_DOWN + L.unit0 + blk * U + (e + 1) * L.chunks)
                    y = bank[4 + (k * X + e) % 2][:, :]
                    if e == 0:
                        to = acc[:, k, :]
                    else:
                        to = yg[:, e % 2, :]
                        done = blk * (X - 1) + e - 1
                        dve.wait_ge(f_acc, FREE_ACC + L.adds + (done - 1 if e > 2 else blk * (X - 1)))
                    if e < L.gated0:
                        dve.tensor_scalar(to, y, tg[:, L.g:L.g + 1], None, ALU.mult).then_inc(f_yg, 1)
                    else:
                        dve.wait_ge(f_gbc, L.gates + blk * E + (e - L.gated0) + 1)
                        dve.tensor_tensor(to, y, g_bc[:, (k * X + e) % 2, :], ALU.mult).then_inc(f_yg, 1)

                def x_add(n):
                    dve.wait_ge(f_at, L.blocks + n + 1)
                    xs = x[:, ds(n * 4, 4), :]
                    dve.tensor_tensor(xs, bank[7][:, :].rearrange("p (t d) -> p t d", t=4), xs, ALU.add)\
                       .then_inc(f_x, 1)

                def slot(blk, u, k, more, after_one):
                    n = blk * U + u
                    hidden(n, u, k)
                    if u >= 1:
                        h_low(n - 1, u - 1, k)
                    elif after_one:
                        h_low(n - 1, U - 1, 1 - k)
                    if after_one and u == X_ADD:
                        x_add(blk - 1)
                    if u >= LAG:
                        if L.plan[u - LAG][1] == L.chunks - 1:
                            weigh_expert(blk, L.plan[u - LAG][0], k)
                    elif after_one and u == LAG - 1:
                        weigh_expert(blk - 1, X - 1, 1 - k)
                    if more and u == STATS:
                        stats(blk + 1)
                    if more and u == GUESS:
                        rsqrt_guess(dve, mv[:, :, 1], 4, 1.0, LN_EPS)
                    if more and u in NEWTON:
                        rsqrt_step(dve, 4)
                    if more and u == ROWS_IN:
                        rows_in(blk + 1)
                    if more and u == X_LO:
                        x_lo(blk + 1, 1 - k)
                    if more and u == LOGITS_IN:
                        logits_in(blk + 1)
                    if more and u == RANK:
                        rank(blk + 1)
                    if more and u == WEIGHTS:
                        weights(blk + 1)
                    if L is L0 and not more and k == 1 and u == STATS:
                        c_rows(0)
                    if L is L0 and not more and k == 1 and u == X_LO:
                        c_inputs(0, 0)

                dve_own.start(0, 0)
                x_lo(0, 0)
                logits_in(0)
                rank(0)
                weights(0)
                dve_own.settle()
                for u in range(ROT):
                    slot(0, u, 0, True, False)
                dve_own.settle()
                with dve.Fori(0, NBLK // 2 - 1) as i:
                    dve_own.start(i, 2 * PREP)
                    for j in range(ROT, 2 * U + ROT):
                        slot(2 * i + j // U, j % U, j // U % 2, True, True)
                    dve_own.end_body()
                dve_own.end(NBLK // 2 - 1)
                dve_own.start(0, 0)
                for j in range(ROT, 2 * U):
                    slot(NBLK - 2 + j // U, j % U, j // U % 2, j < U, True)
                h_low(NBLK * U - 1, U - 1, 1)
                weigh_expert(NBLK - 1, X - 1, 1)
                x_add(NBLK - 1)
                dve_own.settle()

            def c_rows(n):
                for t in range(2):
                    ins_ = dve.bn_stats(stat[:, t, :], x[:, ds(n * 2 + t, 1), :].rearrange("p a d -> p (a d)"))
                link(ins_)
                waited()
                for t in range(2):
                    ins_ = dve.bn_aggr(mv[:, t, :], stat[:, t, :])
                link(ins_)
                r = rsqrt(dve, mv[:, 0:2, 1], 2, 1.0 + LN_EPS, LN_EPS * LN_EPS)
                for t in range(2):
                    ins_ = dve.tensor_scalar(latn[:, t, :], x[:, ds(n * 2 + t, 1), :].rearrange("p a d -> p (a d)"),
                                             mv[:, t, 0:1], r[:, t:t + 1], ALU.subtract, ALU.mult)
                ins_.then_inc(c_xn, 1)

            def c_inputs(n, par):
                dve.wait_ge(c_hi, n + 1)
                dve.tensor_tensor(kv_lo[:, par, 0:NT], lat32[:, :], kv_hi[:, par, 0:NT].bitcast(F32), ALU.subtract)
                dve.tensor_copy(kv_lo[:, par, NT:KEYS], ctx_lo[:, ds(n * NCTX, NCTX)].bitcast(F32)).then_inc(c_lo, 1)

            def c_sum(n, j):
                r = TILE_ROWS[j if j < 2 else j - 2]
                dve.wait_ge(c_sq, 5 * n + j + 1)
                dve.tensor_reduce(ss[0:r, j, :], sq[0:r, :].rearrange("p (h c) -> p h c", h=H1), AX.X, ALU.add)\
                   .then_inc(c_ss, 1)

            def c_norms(n):
                dve.wait_ge(c_ss, 5 * n + 5)
                rsqrt(dve, ss[:, :, :].rearrange("p j h -> p (j h)"), 40, 0.0, 0.0, least=1e-24, buf=rs_qk)

            def c_keys_normed(n):
                y = rs_qk[:, 1, :]
                dve.wait_ge(c_qk, 5 * n + 5)
                for t in range(3):
                    r = TILE_ROWS[t]
                    k3 = k32[0:r, t, :].rearrange("p (h c) -> p h c", h=H1)
                    inv = y[0:r, (2 + t) * H1:(3 + t) * H1].unsqueeze(2).to_broadcast([r, H1, C1])
                    ins_ = dve.tensor_tensor(k3, k3, inv, ALU.mult)
                ins_.then_inc(c_kn, 1)

            def c_rq_in(n):
                if n_from(n, 1):
                    dve.wait_ge(c_exp, 8 * n)
                dve.tensor_copy(rq[:, :, :].rearrange("p t h -> p (t h)"), rs_qk[:, 1, 0:16]).then_inc(c_rq, 1)

            def c_value_in(n, par, t):
                r = TILE_ROWS[t]
                if n_from(n, 2):
                    dve.wait_ge(c_pv, 4 * n - 4)
                dve.wait_ge(c_proj, 8 * n + 6 + t)
                dve.tensor_copy(v32[0:r, par, t, :], bank[5 + (5 + t) % 2][0:r, :]).then_inc(c_v, 1)

            def c_mask_row(n):
                dve.tensor_scalar(key_row[:, NT:KEYS], kmask[:, ds(n, 1), :].rearrange("p a j -> p (a j)"), 1.0,
                                  -NEG / 2, ALU.subtract, ALU.mult)\
                   .then_inc(dve_own.sem, 1)
                dve_own.k += 1

            def c_masked(n, g, half):
                m = 4 * n + g
                small = smx if g % 2 == 0 else smx2
                if n_from(n, 1) or m >= 2:
                    dve.wait_ge(c_pt, 3 * (m - 1))
                for it in (2 * half, 2 * half + 1):
                    z = 4 * g + it
                    dve.wait_ge(c_s, 16 * n + z + 1)
                    waited(it)
                    dve.tensor_tensor_reduce(sc[:, g % 2, it, :], bank[z % 2][:, 0:KEYS], key_row[:, :], 1.0, NEG,
                                             ALU.add, ALU.max, small[:, 0, it:it + 1]).then_inc(c_sm, 1)
                if g == 0 and half == 0:
                    c_rq_in(n)
                    dve.wait_ge(c_rq, n + 1)
                dve.wait_ge(c_sm, 16 * n + 4 * g + 2 * half + 2)
                dve.scalar_tensor_tensor(out=small[:, 1, 2 * half:2 * half + 2], in0=small[:, 0, 2 * half:2 * half + 2],
                                         scalar=-1.0, in1=rq[:, :, 2 * g + half], op0=ALU.mult, op1=ALU.mult)\
                   .then_inc(c_nb, 1)

            def c_p_in(n, g):
                m = 4 * n + g
                if n_from(n, 1) or m > 0:
                    dve.wait_ge(c_pv, m)
                dve.wait_ge(c_pt, 3 * m + 2)
                dve.tensor_copy(pcT[:, 1, :], bank[2 + (3 * g + 1) % 2][:, :]).then_inc(c_pT1, 1)

            def c_o_in(n, g):
                m = 4 * n + g
                small = smx if g % 2 == 0 else smx2
                dve.wait_ge(c_pv, m + 1)
                link(dve.reciprocal(small[:, 3, :], small[:, 2, :]))
                if not isinstance(n, int) or m >= 2:
                    dve.wait_ge(c_ot, m - 1)
                inv = small[:, 3, :].rearrange("p (h t) -> p h t", h=2).unsqueeze(3).to_broadcast([P, 2, 2, C1])
                dve.tensor_tensor(on1[:, g % 2, :, :].rearrange("p t (h c) -> p h t c", h=2),
                                  bank[4][:, 0:4 * C1].rearrange("p (h t c) -> p h t c", h=2, t=2), inv, ALU.mult)\
                   .then_inc(c_on, 1)

            def c_out_in(n):
                dve.wait_ge(c_y, n + 1)
                dve.tensor_copy(yn[:, :, :].rearrange("p a b -> p (a b)"), bank[7][:, 0:NT]).then_inc(c_yd, 1)

            def c_add(n):
                dve.wait_ge(c_yd, n + 1)
                for t in range(2):
                    ins_ = dve.bn_stats(stat[:, 2 + t, :], yn[:, t, :])
                link(ins_)
                waited()
                for t in range(2):
                    ins_ = dve.bn_aggr(mv[:, 2 + t, :], stat[:, 2 + t, :])
                link(ins_)
                r = rsqrt(dve, mv[:, 2:4, 1], 2, 1.0, LN_EPS)
                for t in range(2):
                    ins_ = dve.tensor_scalar(yn[:, t, :], yn[:, t, :], mv[:, 2 + t, 0:1], r[:, t:t + 1],
                                             ALU.subtract, ALU.mult)
                link(ins_)
                link(dve.tensor_tensor(yn[:, :, :], yn[:, :, :], wide(lno[:, 0, :], 2), ALU.mult))
                link(dve.tensor_tensor(yn[:, :, :], yn[:, :, :], wide(lno[:, 1, :], 2), ALU.add))
                xs = x[:, ds(n * 2, 2), :]
                dve.tensor_tensor(xs, xs, yn[:, :, :], ALU.add)

            def c_slot(n, g, ahead, before, first, second):
                if before:
                    c_o_in(*before)
                if ahead:
                    c_masked(*ahead, 0)
                first()
                c_p_in(n, g)
                if ahead:
                    c_masked(*ahead, 1)
                second()

            def c_slot0(n, par, more, first_one):
                def first():
                    c_value_in(n, par, 2)

                def second():
                    if more:
                        for j in range(3):
                            c_sum(n + 1, j)
                c_slot(n, 0, (n, 1), None if first_one else (n - 1, 3), first, second)

            def c_body(n, par, more, more2):
                def first1():
                    if more:
                        c_sum(n + 1, 3)
                        c_sum(n + 1, 4)
                    if n_from(n, 1):
                        c_out_in(n - 1)

                def second1():
                    if more:
                        c_norms(n + 1)
                    else:
                        first_rows()
                c_slot(n, 1, (n, 2), (n, 0), first1, second1)
                c_slot(n, 2, (n, 3), (n, 1), lambda: c_keys_normed(n + 1) if more else None,
                       lambda: c_rows(n + 2) if more2 else None)
                if more:
                    c_mask_row(n + 1)
                    dve.wait_ge(dve_own.sem, dve_own.value())

                def second3():
                    if more:
                        c_value_in(n + 1, 1 - par, 0)
                        c_value_in(n + 1, 1 - par, 1)
                    if more2:
                        c_inputs(n + 2, par)
                    if n_from(n, 1):
                        c_add(n - 1)
                c_slot(n, 3, (n + 1, 0) if more else None, (n, 2), nothing, second3)
                if more:
                    c_slot0(n + 1, 1 - par, more2, False)
                else:
                    c_o_in(n, 3)
                    c_out_in(n)
                    c_add(n)

            def pass_c():
                dve_own.start(0, 0)
                link(dve.memset(key_row[:, :], 0.0))
                link(dve.memset(ss[:, :, :], 1.0))
                for k, name in enumerate(("ln_o_w", "ln_o_b")):
                    link(dve.tensor_scalar(lno[:, k, :], row(name), tg[:, 1:2], None, ALU.mult))
                dve.tensor_scalar(qks[:, :], col("q_scale"), col("k_scale"), float(C1 ** 0.5), ALU.mult, ALU.mult)\
                   .then_inc(c_setup, 1)
                c_rows(1)
                for j in range(5):
                    c_sum(0, j)
                c_norms(0)
                c_keys_normed(0)
                c_mask_row(0)
                dve.wait_ge(dve_own.sem, dve_own.value())
                c_value_in(0, 0, 0)
                c_value_in(0, 0, 1)
                c_inputs(1, 1)
                c_masked(0, 0, 0)
                c_masked(0, 0, 1)
                c_slot0(0, 0, True, True)
                c_body(0, 0, True, True)
                dve_own.settle()
                steps = RSQRT_STEPS + 4 + (2 + RSQRT_STEPS) + 1 + (2 + RSQRT_STEPS + 3)
                with dve.Fori(0, (NB - 4) // 2) as i:
                    dve_own.start(i, 2 * steps)
                    c_body(2 * i + 1, 1, True, True)
                    c_body(2 * i + 2, 0, True, True)
                    dve_own.end_body()
                dve_own.end((NB - 4) // 2)
                dve_own.start(0, 0)
                c_body(NB - 3, 1, True, True)
                c_body(NB - 2, 0, True, False)
                c_body(NB - 1, 1, False, False)
                dve_own.settle()

            ffn(L0)
            pass_c()
            ffn(L1)


def kernel(**inputs):
    import concourse.bacc as bacc
    from concourse.bass_utils import run_bass_kernel_spmd as run

    arrays = lay_out({k: np.asarray(v) for k, v in inputs.items()})
    nc = bacc.Bacc("TRN2", target_bir_lowering=False, num_devices=1)
    ins = {k: nc.dram_tensor(f"in_{k}", a.shape, mybir.dt.from_np(a.dtype), kind="ExternalInput").ap()
           for k, a in arrays.items()}
    out = nc.dram_tensor("out_x", (NB * NT, P), F32, kind="ExternalOutput").ap()
    build(nc, ins, out)
    r = run(nc, [{f"in_{k}": a for k, a in arrays.items()}], core_ids=[0])
    return r.results[0]["out_x"].reshape(NB, NT, P)
```
